# Optimizing a Trainium2 kernel written in Bass

```python
import numpy as np
import jax
import jax.numpy as jnp

def _softmax(x, axis=-1):
    return jax.nn.softmax(x, axis=axis)

def _gelu(x):
    return jax.nn.gelu(x, approximate=True)

def _silu(x):
    return jax.nn.silu(x)

def _sigmoid(x):
    return jax.nn.sigmoid(x)

def _layernorm(x, axis=-1, eps=1e-05):
    m = jnp.mean(x, axis=axis, keepdims=True)
    v = jnp.var(x, axis=axis, keepdims=True)
    return (x - m) / jnp.sqrt(v + eps)

def _scatter_add(tgt, idx, src, axis=0):
    return tgt.at[idx].add(src)

def _segment_sum(src, seg, n):
    return jax.ops.segment_sum(src, seg, n)
kernel_name = 'mk_xattn_ffn_d1_seqx_r8_134eed'

def setup_inputs(seed: int=0):
    np.random.seed(seed)
    _w = jnp.asarray

    def _rec_inputs():
        import jax
        import jax.numpy as jnp
        _rk = jax.random.key(seed)
        x = -0.0003929 + 0.9999 * jax.random.normal(jax.random.fold_in(_rk, 1), (2, 256, 256), jnp.float32)
        _lenS = 256 - jax.random.randint(jax.random.fold_in(_rk, 7), (2,), 0, max(1, 256 // 4) + 1, jnp.int32)
        _lenS2 = 512 - jax.random.randint(jax.random.fold_in(_rk, 8), (2,), 0, max(1, 512 // 4) + 1, jnp.int32)
        _ctx_2048P = jax.random.normal(jax.random.fold_in(_rk, 11), (2, 16, 256), jnp.float32)
        _ctx_2048c = jax.random.dirichlet(jax.random.fold_in(_rk, 511), 0.3 * jnp.ones((16,), jnp.float32), (2, 512))
        _ctx_2048t = jnp.einsum('bsk,bkd->bsd', _ctx_2048c, _ctx_2048P)
        _ctx_2048t = _ctx_2048t * jax.lax.rsqrt(jnp.mean(jnp.square(_ctx_2048t)) + 1e-12) * 0.953939
        ctx_2048 = -0.000514642 + 1.00011 * (_ctx_2048t + 0.3 * jax.random.normal(jax.random.fold_in(_rk, 611), (2, 512, 256), jnp.float32))
        _validS = jnp.arange(256)[None, :] < _lenS[:, None]
        _validS2 = jnp.arange(512)[None, :] < _lenS2[:, None]
        _causal = jnp.tril(jnp.ones((256, 256), dtype=bool))
        mask_BxSxS2_ff0 = jnp.where(jnp.ones((2, 256, 512), dtype=bool), 0.0, -1000000000.0).astype(jnp.float32)
        return (x, ctx_2048, mask_BxSxS2_ff0)
    x, ctx_2048, mask_BxSxS2_ff0 = _rec_inputs()

    def _L0_xattn_setup():
        import jax, jax.numpy as jnp
        import numpy as np
        NUM_HEADS = 16
        EPS = 1e-08

        def _dyn_quant(x):
            s = jnp.maximum(jnp.max(jnp.abs(x), axis=-1, keepdims=True) / 127.0, EPS)
            q = jnp.clip(jnp.round(x / s), -127.0, 127.0)
            return (q, s)

        def _quant_weight(w):
            s = jnp.maximum(jnp.max(jnp.abs(w), axis=1, keepdims=True) / 127.0, EPS)
            q = jnp.clip(jnp.round(w / s), -127.0, 127.0)
            return (q, s)

        def _w8a8_linear(x, w, b):
            qx, sx = _dyn_quant(x)
            qw, sw = _quant_weight(w)
            y = jnp.einsum('bnc,oc->bno', qx, qw) * (sx * sw[:, 0])
            return y + b
        key = jax.random.key(seed)
        ks = jax.random.split(key, 9)
        B, N, L, C = (2, 512, 64, 256)
        sc = 0.02
        return {'x': jax.random.normal(ks[0], (B, N, C), jnp.float32), 'cond': jax.random.normal(ks[1], (B, L, C), jnp.float32), 'mask': jnp.zeros((B, N, L), jnp.float32), 'wq': jax.random.normal(ks[2], (C, C), jnp.float32) * sc, 'bq': jnp.zeros((C,), jnp.float32), 'wk': jax.random.normal(ks[3], (C, C), jnp.float32) * sc, 'bk': jnp.zeros((C,), jnp.float32), 'wv': jax.random.normal(ks[4], (C, C), jnp.float32) * sc, 'bv': jnp.zeros((C,), jnp.float32), 'wo': jax.random.normal(ks[5], (C, C), jnp.float32) * sc, 'bo': jnp.zeros((C,), jnp.float32)}
    _L0_xattn_all = _L0_xattn_setup()
    _L0_xattn_in = {k: v for k, v in _L0_xattn_all.items() if k in ('wq', 'bq', 'wk', 'bk', 'wv', 'bv', 'wo', 'bo')}
    del _L0_xattn_all

    def _L0_ffn_setup():
        import jax, jax.numpy as jnp
        import numpy as np
        NUM_EXPERTS = 32
        TOP_K = 8
        THRESHOLD = 0.8
        HIDDEN = 256
        INTER = 96
        key = jax.random.key(seed)
        k1, k2, k3, k4 = jax.random.split(key, 4)
        hidden_states = jax.random.normal(k1, (2, 128, HIDDEN), jnp.float32)
        gate_weight = jax.random.normal(k2, (NUM_EXPERTS, HIDDEN), jnp.float32) * 0.02
        gate_up_proj = jax.random.normal(k3, (NUM_EXPERTS, 2 * INTER, HIDDEN), jnp.float32) * 0.02
        down_proj = jax.random.normal(k4, (NUM_EXPERTS, HIDDEN, INTER), jnp.float32) * 0.02
        return {'hidden_states': hidden_states, 'gate_weight': gate_weight, 'gate_up_proj': gate_up_proj, 'down_proj': down_proj}
    _L0_ffn_all = _L0_ffn_setup()
    _L0_ffn_in = {k: v for k, v in _L0_ffn_all.items() if k in ('gate_weight', 'gate_up_proj', 'down_proj')}
    del _L0_ffn_all
    return {'x': x, 'ctx_2048': ctx_2048, 'mask_BxSxS2_ff0': mask_BxSxS2_ff0, 'L0_xattn_wq': _L0_xattn_in['wq'], 'L0_xattn_bq': _L0_xattn_in['bq'], 'L0_xattn_wk': _L0_xattn_in['wk'], 'L0_xattn_bk': _L0_xattn_in['bk'], 'L0_xattn_wv': _L0_xattn_in['wv'], 'L0_xattn_bv': _L0_xattn_in['bv'], 'L0_xattn_wo': _L0_xattn_in['wo'], 'L0_xattn_bo': _L0_xattn_in['bo'], 'L0_ffn_gate_weight': _L0_ffn_in['gate_weight'], 'L0_ffn_gate_up_proj': _L0_ffn_in['gate_up_proj'], 'L0_ffn_down_proj': _L0_ffn_in['down_proj']}

def reference(x, ctx_2048, mask_BxSxS2_ff0, L0_xattn_wq, L0_xattn_bq, L0_xattn_wk, L0_xattn_bk, L0_xattn_wv, L0_xattn_bv, L0_xattn_wo, L0_xattn_bo, L0_ffn_gate_weight, L0_ffn_gate_up_proj, L0_ffn_down_proj):
    import jax
    import jax.numpy as jnp

    def _L0_xattn_ref(x, cond, mask, wq, bq, wk, bk, wv, bv, wo, bo):
        import jax, jax.numpy as jnp
        import numpy as np
        NUM_HEADS = 16
        EPS = 1e-08

        def _dyn_quant(x):
            s = jnp.maximum(jnp.max(jnp.abs(x), axis=-1, keepdims=True) / 127.0, EPS)
            q = jnp.clip(jnp.round(x / s), -127.0, 127.0)
            return (q, s)

        def _quant_weight(w):
            s = jnp.maximum(jnp.max(jnp.abs(w), axis=1, keepdims=True) / 127.0, EPS)
            q = jnp.clip(jnp.round(w / s), -127.0, 127.0)
            return (q, s)

        def _w8a8_linear(x, w, b):
            qx, sx = _dyn_quant(x)
            qw, sw = _quant_weight(w)
            y = jnp.einsum('bnc,oc->bno', qx, qw) * (sx * sw[:, 0])
            return y + b
        B, N, C = x.shape
        L = cond.shape[1]
        H = NUM_HEADS
        D = C // H
        inv_sqrt_d = np.float32(1.0 / np.sqrt(D))
        q = _w8a8_linear(x, wq, bq).reshape(B, N, H, D).transpose(0, 2, 1, 3)
        k = (cond @ wk.T + bk).reshape(B, L, H, D).transpose(0, 2, 1, 3)
        v = (cond @ wv.T + bv).reshape(B, L, H, D).transpose(0, 2, 1, 3)
        scores = jnp.einsum('bhnd,bhld->bhnl', q, k) * inv_sqrt_d + mask[:, None]
        attn = jax.nn.softmax(scores, axis=-1)
        o = jnp.einsum('bhnl,bhld->bhnd', attn, v)
        o = o.transpose(0, 2, 1, 3).reshape(B, N, C)
        return _w8a8_linear(o, wo, bo)

    def _L0_ffn_ref(hidden_states, gate_weight, gate_up_proj, down_proj):
        import jax, jax.numpy as jnp
        import numpy as np
        NUM_EXPERTS = 32
        TOP_K = 8
        THRESHOLD = 0.8
        HIDDEN = 256
        INTER = 96
        B, S, H = hidden_states.shape
        x = hidden_states.reshape(-1, H)
        logits = x @ gate_weight.T
        probs = jax.nn.softmax(logits.astype(jnp.float32), axis=-1).astype(logits.dtype)
        top_vals, top_idx = jax.lax.top_k(probs, TOP_K)
        renorm = top_vals / jnp.clip(jnp.sum(top_vals, axis=-1, keepdims=True), 1e-12)
        cum = jnp.cumsum(renorm, axis=-1)
        num_keep = jnp.minimum(jnp.sum((cum < THRESHOLD).astype(jnp.int32), axis=-1) + 1, TOP_K)
        active = jnp.arange(TOP_K)[None, :] < num_keep[:, None]
        rw = top_vals * active.astype(top_vals.dtype)
        rw = rw / jnp.clip(jnp.sum(rw, axis=-1, keepdims=True), 1e-12)
        combine = jnp.sum(jax.nn.one_hot(top_idx, NUM_EXPERTS, dtype=rw.dtype) * rw[..., None], axis=1)

        def body(acc, params):
            w_gu, w_d, ce = params
            gu = x @ w_gu.T
            g, u = jnp.split(gu, 2, axis=-1)
            h = jax.nn.silu(g) * u
            return (acc + h @ w_d.T * ce[:, None], None)
        out, _ = jax.lax.scan(body, jnp.zeros_like(x), (gate_up_proj, down_proj, combine.T))
        return out.reshape(B, S, H)
    x = x + _L0_xattn_ref(_layernorm(x, axis=-1), ctx_2048, mask_BxSxS2_ff0, L0_xattn_wq, L0_xattn_bq, L0_xattn_wk, L0_xattn_bk, L0_xattn_wv, L0_xattn_bv, L0_xattn_wo, L0_xattn_bo)
    x = x + _L0_ffn_ref(_layernorm(x, axis=-1), L0_ffn_gate_weight, L0_ffn_gate_up_proj, L0_ffn_down_proj)
    return x

_drawn_inputs = setup_inputs


def setup_inputs(seed=0):
    import zlib

    import numpy as np

    out = dict(_drawn_inputs(seed))
    spreads = {'L0_xattn_bq': (0.0, 0.8),
     'L0_xattn_bk': (0.0, 0.8),
     'L0_xattn_bv': (0.0, 0.1),
     'L0_xattn_bo': (0.0, 0.1)}
    factors = {'L0_xattn_wq': 8.0,
     'L0_xattn_wk': 8.0,
     'L0_ffn_gate_weight': 8.0,
     'L0_ffn_gate_up_proj': 8.0,
     'L0_ffn_down_proj': 8.0}
    for name, (base, spread) in spreads.items():
        noise = np.random.default_rng([zlib.crc32(name.encode()), seed]).standard_normal(out[name].shape)
        drawn = base * np.exp(spread * noise) if base else spread * noise
        out[name] = jnp.asarray(drawn.astype(out[name].dtype))
    for name, factor in factors.items():
        out[name] = (out[name] * factor).astype(out[name].dtype)
    return out
```

```python
from contextlib import ExitStack

import concourse.bass as bass
from concourse import mybir

F32 = mybir.dt.float32
F32R = mybir.dt.float32r
BF16 = mybir.dt.bfloat16
ALU = mybir.AluOpType
ACT = mybir.ActivationFunctionType
AX = mybir.AxisListType

P = 128
B, N, L, C = 2, 256, 512, 256
H = 16
D = C // H
TOK = B * N
NT = TOK // P
NTB = N // P
CK = C // P
LC = L // P
HG = 4
G = H // HG
GC = HG * D
E, INTER, TOPK = 32, 96, 8
FT = E * INTER // P
WGU = CK * 2 * P
WRAW = WGU + C
PV = D + 1
KEEP = 0.8
LN_EPS = 1e-5
Q_EPS = 1e-8
QMAX = 127.0
ROUND = 12582912.0
BIG = 3.0e38


def build(nc, x, ctx_t, mask, wq, bq_t, wk_t, bk_t, wv_t, bv, wo, bo, gate_t, gu_t, down_t, out):
    with ExitStack() as stack:
        def sem(name):
            return stack.enter_context(nc.semaphore(name))

        def sb_in(scope, name, shape, dt=F32):
            return scope.enter_context(nc.sbuf_tensor(name, shape, dt))

        def sb(name, shape, dt=F32):
            return sb_in(stack, name, shape, dt)

        ident = sb("ident", [P, P])
        ident_bf = sb("ident_bf", [P, P], BF16)
        ones_row = sb("ones_row", [1, P])
        head_band = sb("head_band", [P, 2, H])
        head_mask = sb("head_mask", [P, H])
        part_col = sb("part_col", [P, 1])
        part_step = sb("part_step", [P, 2])
        part_mod = sb("part_mod", [P, 1])
        expert_sel = sb("expert_sel", [P, FT * P], BF16)
        x_sb = sb("x_sb", [P, NT, C])
        x_bo = sb("x_bo", [P, NT, C])
        x2 = sb("x2", [P, NT, C])
        xn = sb("xn", [P, NT, C])
        wo_sb = sb("wo_sb", [P, CK, C])
        woq = sb("woq", [P, CK, C], BF16)
        woq_t = sb("woq_t", [P, CK, C], BF16)
        wo_scale = sb("wo_scale", [P, C])
        gate_sb = sb("gate_sb", [P, CK, E])
        bq_sb = sb("bq_sb", [P, G])
        bk_sb = sb("bk_sb", [P, G])
        bo_sb = sb("bo_sb", [P, C])
        ln_stats = sb("ln_stats", [P, 2, NT, 6])
        ln_mv = sb("ln_mv", [P, 2, NT, 2])
        ln_var = sb("ln_var", [P, 2, NT])
        ln_std = sb("ln_std", [P, 2, NT])
        ln_rstd = sb("ln_rstd", [P, 2, NT])
        amax = sb("amax", [P, 4, NT])
        scale = sb("scale", [P, 4, NT])
        rscale = sb("rscale", [P, 4, NT])
        neg_max = sb("neg_max", [P, NT])
        rsum = sb("rsum", [P, NT, H])
        r_max = sb("r_max", [P, NT])
        r_sum = sb("r_sum", [P, 3, NT])
        r_p = sb("r_p", [P, NT, E + TOPK])
        r_act = sb("r_act", [P, NT, TOPK])
        r_zero = sb("r_zero", [P, TOPK])

        q_scale = sb("q_scale", [P, 2, TOK])
        q_f = sb("q_f", [P, 2, TOK])

        first = ExitStack()

        def sb(name, shape, dt=F32):
            return sb_in(first, name, shape, dt)

        expert_of = sb("expert_of", [P, FT * P], BF16)
        ctx_sb = sb("ctx_sb", [P, CK, B * L])
        ctx_hi = sb("ctx_hi", [P, CK, B * L], F32R)
        ctx_lo = sb("ctx_lo", [P, CK, B * L], F32R)
        wq_sb = sb("wq_sb", [P, CK, C])
        wk_sb = sb("wk_sb", [P, CK, C])
        wk_hi = sb("wk_hi", [P, CK * G, 2, GC], F32R)
        wk_lo = sb("wk_lo", [P, CK * G, 2, GC], F32R)
        wv_sb = sb("wv_sb", [P, CK, C])
        wv_hi = sb("wv_hi", [P, CK, C], F32R)
        wv_lo = sb("wv_lo", [P, CK, C], F32R)
        bv_sb = sb("bv_sb", [P, C])
        key_f = sb("key_f", [P, 2, L])
        xq = sb("xq", [P, NT, C], BF16)
        xq_t = sb("xq_t", [P, CK, TOK], BF16)
        wqq = sb("wqq", [P, CK, C], BF16)
        wqq_t = sb("wqq_t", [P, CK * G, 2, GC], BF16)
        x_scale_row = sb("x_scale_row", [1, TOK])
        wq_scale_row = sb("wq_scale_row", [1, G, 2, GC])
        wo_scale_row = sb("wo_scale_row", [1, C])
        first.close()

        w_raw_gu = sb_in(stack, "w_raw_gu", [P, FT, WGU])
        w_raw_dn = sb_in(stack, "w_raw_dn", [P, FT, C])

        second = ExitStack()

        def sb(name, shape, dt=F32):
            return sb_in(second, name, shape, dt)

        mask_sb = sb("mask_sb", [P, NT, L])
        key = sb("key", [P, G * B * L], F32R)
        val = sb("val", [P, B, LC, H, PV])
        q_hi = sb("q_hi", [P, G * TOK], F32R)
        q_lo = sb("q_lo", [P, G * TOK], F32R)
        qm_hi = sb("qm_hi", [P, TOK], F32R)
        qm_lo = sb("qm_lo", [P, TOK], F32R)
        neg_s = sb("neg_s", [P, NT, L])
        prob = sb("prob", [P, NT, L])
        prob_t = sb("prob_t", [P, NT, L])
        second.close()

        def sb(name, shape, dt=F32):
            return sb_in(stack, name, shape, dt)

        o_sb = sb("o_sb", [P, NT, C])
        oq = sb("oq", [P, NT, C], BF16)
        oq_t = sb("oq_t", [P, NT, CK, P], BF16)
        proj = sb("proj", [P, NT, C])
        xn_t = sb("xn_t", [P, CK, TOK])
        xn_hi = sb("xn_hi", [P, CK, TOK], F32R)
        xn_lo = sb("xn_lo", [P, CK, TOK], F32R)
        r_e = sb("r_e", [P, NT, E])
        r_top = sb("r_top", [P, NT, TOPK])
        r_ren = sb("r_ren", [P, NT, TOPK])
        r_cum = sb("r_cum", [P, NT, TOPK])
        r_rw = sb("r_rw", [P, NT, TOPK])
        r_find = sb("r_find", [P, NT, TOPK])
        r_rep = sb("r_rep", [P, NT, E + TOPK])
        comb = sb("comb", [P, NT, E])
        comb3 = sb("comb3", [P, NT, 3, E])
        comb_t = sb("comb_t", [P, TOK])
        comb_part = sb("comb_part", [P, TOK], BF16)
        w_hi_gu = sb("w_hi_gu", [P, 2, WGU], F32R)
        w_lo_gu = sb("w_lo_gu", [P, 2, WGU], F32R)
        w_hi_dn = sb("w_hi_dn", [P, 2, C], F32R)
        w_lo_dn = sb("w_lo_dn", [P, 2, C], F32R)
        silu = sb("silu", [P, 2, TOK])
        gated = sb("gated", [P, 2, TOK])
        hid = sb("hid", [P, 2, TOK])
        hid_hi = sb("hid_hi", [P, 2, TOK], F32R)
        hid_lo = sb("hid_lo", [P, 2, TOK], F32R)
        y_sb = sb("y_sb", [P, NT, C])

        ps = stack.enter_context(nc.psum_tensor("ps", [P, 8, 512], F32))

        def bank(i, n=512, rows=P):
            return ps[0:rows, i, 0:n]

        def bank_bf(i, n):
            return ps[:, i, 0:n // 2].bitcast(BF16)

        loads = ["x", "ctx0", "ctx1", "mask", "wq", "wo", "wk", "wv", "bq", "bk", "bv", "bo", "gate"]
        ld = {n: sem("ld_" + n) for n in loads}
        NGU = 4
        ld_gu = [sem(f"ld_gu{i}") for i in range(NGU)]
        ld_dn = sem("ld_dn")
        names = """ce_mm comb comb_part comb_sb comb_tp const_ident const_mask const_pad const_sel
            ctx_hi ctx_lo dn_mm dn_split dve_step expd g_mm gated gu_split hid hid_hi hid_lo
            k_act k_done k_mm lg_exp lg_mm lg_sub o_mm o_read oq oq_t oq_tp outer_mm pool_hi
            pool_step pt_act pt_dve pt_mm pv q_acc_read q_done q_mm qm qs_sb row_tp rows score
            sel silu sm sm_turn pool_turn std stored u_mm v_done v_mm var w_tp wk_hi wk_lo wo_sc wo_sc_mm woq
            woq_t wqq wqq_t wv_hi wv_lo x_bo xn1 xn2 xn_hi xn_lo xn_tp xq xq_t xq_tp y_done y_mm""".split()
        s = {n: sem("s_" + n) for n in names}

        block = stack.enter_context(nc.Block())

        def twice(ap):
            ap = ap.rearrange("p (g c) -> p g c", c=GC)
            return ap.unsqueeze(2).to_broadcast([ap.shape[0], ap.shape[1], 2, GC])

        def group_at(h, width, start, n):
            return bass.ds((h & (H - HG)) * (width // HG) + start, n)

        def fr(ap):
            return ap.bitcast(F32)

        def wait(eng, name, count):
            if not isinstance(count, int) or count > 0:
                eng.wait_ge(s[name], count)

        x_dram = x.rearrange("(t p) c -> p t c", p=P)
        ctx_dram = ctx_t.rearrange("(k p) n -> p k n", p=P)
        out_dram = out.rearrange("b (t p) c -> p (b t) c", p=P)

        @block.sync
        def _(sp):
            sp.dma_start(x_sb[:], x_dram).then_inc(ld["x"], 16)
            sp.dma_start(ctx_sb[:, :, 0:L], ctx_dram[:, :, 0:L]).then_inc(ld["ctx0"], 16)
            sp.dma_start(wv_sb[:], wv_t.rearrange("(k p) n -> p k n", p=P)).then_inc(ld["wv"], 16)
            sp.dma_start(bv_sb[:], bv.partition_broadcast(P)).then_inc(ld["bv"], 16)
            sp.dma_start(mask_sb[:], mask.rearrange("b (t p) l -> p (b t) l", p=P)).then_inc(ld["mask"], 16)
            sp.wait_ge(s["v_done"], B * LC)
            sp.wait_ge(s["k_done"], G * B)
            sp.wait_ge(s["q_done"], G)
            for i in range(NGU):
                cut = slice(i * FT // NGU, (i + 1) * FT // NGU)
                sp.dma_start(w_raw_gu[:, cut, :], gu_t[:, cut, :]).then_inc(ld_gu[i], 16)
                if i == 0:
                    sp.dma_start(w_raw_dn[:], down_t).then_inc(ld_dn, 16)
            for t in range(NT):
                sp.wait_ge(s["y_done"], t + 1)
                sp.dma_start(out_dram[:, t, :], y_sb[:, t, :]).then_inc(s["stored"], 16)
            sp.wait_ge(s["stored"], 16 * NT)

        @block.gpsimd
        def _(pool):
            g = nc.gpsimd
            n = [0]

            def step(ins):
                n[0] += 1
                ins.then_inc(s["pool_step"], 1)
                pool.wait_ge(s["pool_step"], n[0])

            step(g.memset(ident[:], 0.0))
            g.affine_select(out=ident[:], in_=ident[:], compare_op=ALU.not_equal, fill=1.0, base=0,
                            pattern=[[-1, P]], channel_multiplier=1).then_inc(s["const_ident"], 1)
            pool.wait_ge(s["const_ident"], 1)
            g.tensor_copy(ident_bf[:], ident[:]).then_inc(s["const_ident"], 1)
            g.memset(ones_row[:], 1.0).then_inc(s["const_ident"], 1)
            g.iota(expert_of[:], pattern=[[1, E], [0, INTER]], base=0, channel_multiplier=0,
                   allow_small_or_imprecise_dtypes=True)
            step(g.iota(part_col[:], pattern=[[0, 1]], base=0, channel_multiplier=1,
                        allow_small_or_imprecise_dtypes=True))
            step(g.tensor_scalar(part_mod[:], part_col[:], 32.0, -32.0, ALU.is_ge, ALU.mult))
            step(g.tensor_tensor(part_mod[:], part_mod[:], part_col[:], ALU.add))
            step(g.tensor_scalar(part_step[:, 1:2], part_col[:], 64.0, -32.0, ALU.is_ge, ALU.mult))
            step(g.tensor_tensor(part_mod[:], part_mod[:], part_step[:, 1:2], ALU.add))
            g.tensor_scalar(part_step[:, 0:1], part_col[:], 32.0, -1.0, ALU.is_ge, ALU.mult)
            g.tensor_scalar(part_step[:, 1:2], part_col[:], 64.0, -1.0, ALU.is_ge, ALU.mult).then_inc(s["const_sel"], 1)
            g.memset(val[:], 1.0).then_inc(s["const_pad"], 1)

            def low(lo, full, hi, done):
                g.tensor_tensor(lo, full, fr(hi), ALU.subtract).then_inc(s[done], 1)

            for b in range(B):
                for k in range(CK):
                    pool.wait_ge(s["ctx_hi"], b + 1)
                    at = slice(b * L, (b + 1) * L)
                    low(ctx_lo[:, k, at], ctx_sb[:, k, at], ctx_hi[:, k, at], "ctx_lo")

            step(g.memset(head_band[:], 1.0))
            band = head_band[:].rearrange("p d (a h) -> p d a h", h=HG)
            step(g.affine_select(out=band, in_=band, compare_op=ALU.is_ge, fill=0.0, base=0,
                                 pattern=[[-GC, 2], [0, G], [-D, HG]], channel_multiplier=1))
            step(g.affine_select(out=band, in_=band, compare_op=ALU.is_ge, fill=0.0, base=D - 1,
                                 pattern=[[GC, 2], [0, G], [D, HG]], channel_multiplier=-1))
            g.tensor_tensor(head_mask[:], head_band[:, 0, :], head_band[:, 1, :], ALU.add).then_inc(s["const_mask"], 1)
            g.memset(r_zero[:], 0.0)
            g.memset(r_act[:], 1.0)
            g.memset(r_p[:], -1.0).then_inc(s["const_pad"], 1)

            pool.wait_ge(s["const_pad"], 2)
            for i in range(G * B):
                if i == 1:
                    pool.wait_ge(s["k_done"], 1)
                    pool.wait_ge(s["wv_hi"], 1)
                    low(wv_lo[:], wv_sb[:], wv_hi[:], "wv_lo")
                    pool.wait_ge(s["wv_lo"], 1)
                pool.wait_ge(s["k_act"], i + 1)
                lo_rows = key[GC:P, i * L:(i + 1) * L]
                g.tensor_tensor(lo_rows, key_f[GC:P, i % 2, :], fr(lo_rows), ALU.subtract).then_inc(s["k_done"], 1)
            pool.wait_ge(s["k_done"], G * B)

            pool.wait_ge(s["const_mask"], 1)
            pool.wait_ge(s["q_done"], G)

            def mask_query(h, m):
                wait(pool, "score", h * NT + (2 * m + 2 - NT))
                pool.sem_inc(s["pool_turn"], 1)
                pool.sem_inc(s["pool_turn"], 1)
                cols = slice(m * 2 * P, (m + 1) * 2 * P)
                hm = head_mask[:, bass.ds(h, 1)].to_broadcast([P, 2 * P])
                for qm, q in ((qm_hi, q_hi), (qm_lo, q_lo)):
                    ins = g.tensor_tensor(qm[:, cols], fr(q[:, group_at(h, TOK, m * 2 * P, 2 * P)]), hm, ALU.mult)
                ins.then_inc(s["qm"], 1)

            for m in range(NT // 2):
                mask_query(0, m)
            pool.wait_ge(ld["x"], 16)
            pool.wait_ge(ld["bo"], 16)
            g.tensor_tensor(x_bo[:], x_sb[:], bo_sb[:].unsqueeze(1).to_broadcast([P, NT, C]), ALU.add).then_inc(s["x_bo"], 1)
            with pool.Fori(1, H) as h:
                for m in range(NT // 2):
                    mask_query(h, m)

            def split_gu(j, sl):
                wait(pool, "u_mm", j - 1)
                pool.sem_inc(s["pool_turn"], 1)
                raw = w_raw_gu[:, bass.ds(j, 1), :].squeeze(1)
                g.tensor_copy(w_hi_gu[:, sl, :], raw).then_inc(s["pool_hi"], 1)
                pool.wait_ge(s["pool_hi"], 2 * j + 1)
                pool.sem_inc(s["pool_turn"], 1)
                g.tensor_tensor(w_lo_gu[:, sl, :], raw, fr(w_hi_gu[:, sl, :]), ALU.subtract).then_inc(s["gu_split"], 1)

            def split_dn(j, sl):
                wait(pool, "dn_mm", j - 1)
                pool.sem_inc(s["pool_turn"], 1)
                raw = w_raw_dn[:, bass.ds(j, 1), :].squeeze(1)
                g.tensor_copy(w_hi_dn[:, sl, :], raw).then_inc(s["pool_hi"], 1)
                pool.wait_ge(s["pool_hi"], 2 * j + 2)
                pool.sem_inc(s["pool_turn"], 1)
                g.tensor_tensor(w_lo_dn[:, sl, :], raw, fr(w_hi_dn[:, sl, :]), ALU.subtract).then_inc(s["dn_split"], 1)

            pool.wait_ge(s["pv"], H * NT)
            for q in (*ld_gu, ld_dn):
                pool.wait_ge(q, 16)
            for j in range(2):
                split_gu(j, j)
                split_dn(j, j)
            for t in range(NT):
                pool.wait_ge(s["xn_hi"], t + 1)
                at = slice(t * P, (t + 1) * P)
                low(xn_lo[:, :, at], xn_t[:, :, at], xn_hi[:, :, at], "xn_lo")
            with pool.Fori(1, FT // 2) as i:
                for sl in range(2):
                    split_gu(i * 2 + sl, sl)
                    split_dn(i * 2 + sl, sl)

        @block.scalar
        def _(act):
            a = nc.scalar
            dram = lambda w: w.rearrange("(k p) n -> p k n", p=P)
            act.dma_start(wk_sb[:], dram(wk_t)).then_inc(ld["wk"], 16)
            act.dma_start(wq_sb[:], dram(wq)).then_inc(ld["wq"], 16)
            act.dma_start(ctx_sb[:, :, L:2 * L], ctx_dram[:, :, L:2 * L]).then_inc(ld["ctx1"], 16)
            for half in range(2):
                act.dma_start(bk_sb[half * GC:(half + 1) * GC, :], bk_t).then_inc(ld["bk"], 16)
                act.dma_start(bq_sb[half * GC:(half + 1) * GC, :], bq_t).then_inc(ld["bq"], 16)
            act.dma_start(wo_sb[:], dram(wo)).then_inc(ld["wo"], 16)
            act.dma_start(bo_sb[:], bo.partition_broadcast(P)).then_inc(ld["bo"], 16)
            act.dma_start(gate_sb[:], dram(gate_t)).then_inc(ld["gate"], 16)

            act.wait_ge(ld["wk"], 16)
            a.copy(wk_hi[:], twice(wk_sb[:].rearrange("p k c -> p (k c)"))).then_inc(s["wk_hi"], 1)
            act.wait_ge(ld["ctx0"], 16)
            a.copy(ctx_hi[:, :, 0:L], ctx_sb[:, :, 0:L]).then_inc(s["ctx_hi"], 1)
            act.wait_ge(ld["ctx1"], 16)
            a.copy(ctx_hi[:, :, L:2 * L], ctx_sb[:, :, L:2 * L]).then_inc(s["ctx_hi"], 1)
            act.wait_ge(s["var"], 1)
            a.activation(ln_std[:, 0, :], ln_var[:, 0, :], ACT.Sqrt).then_inc(s["std"], 1)
            act.wait_ge(ld["wv"], 16)
            a.copy(wv_hi[:], wv_sb[:]).then_inc(s["wv_hi"], 1)

            act.wait_ge(ld["bk"], 32)

            def key_out(i):
                act.wait_ge(s["k_mm"], i + 1)
                gi = i // B
                a.activation(key[:, i * L:(i + 1) * L], bank(i % 2), ACT.Identity, bias=bk_sb[:, gi:gi + 1])
                if i >= 2:
                    act.wait_ge(s["k_done"], i - 1)
                a.activation(key_f[GC:P, i % 2, :], ps[GC:P, i % 2, :], ACT.Identity,
                             bias=bk_sb[GC:P, gi:gi + 1]).then_inc(s["k_act"], 1)

            for i in range(5):
                key_out(i)
            act.wait_ge(s["xq_tp"], 1)
            a.copy(xq_t[:].rearrange("p k n -> p (k n)"), bank_bf(4, CK * TOK)).then_inc(s["xq_t"], 1)
            act.wait_ge(s["w_tp"], 1)
            a.copy(wqq_t[:], twice(bank_bf(5, CK * C))).then_inc(s["wqq_t"], 1)
            act.wait_ge(s["row_tp"], 1)
            a.copy(x_scale_row[:], bank(6, TOK, 1))
            a.copy(wq_scale_row[:], twice(bank(7, C, 1)))
            a.copy(wo_scale_row[:], ps[0:1, 7, C:2 * C]).then_inc(s["rows"], 1)
            for i in range(5, G * B):
                key_out(i)
            act.wait_ge(s["w_tp"], 2)
            a.copy(woq_t[:].rearrange("p k n -> p (k n)"), bank_bf(4, CK * C)).then_inc(s["woq_t"], 1)
            for i in range(G):
                act.wait_ge(s["outer_mm"], i + 1)
                if i >= 2:
                    act.wait_ge(s["q_acc_read"], i - 1)
                a.copy(q_scale[:, i % 2, :], bank(6 + i % 2)).then_inc(s["qs_sb"], 1)
            act.wait_ge(s["wo_sc_mm"], 1)
            a.copy(wo_scale[:], bank(5, C)).then_inc(s["wo_sc"], 1)

            def exponent(h, t):
                n = h * NT + t
                act.wait_ge(s["sm"], n + 1)
                wait(act, "pt_mm", n - 3)
                a.activation(prob[:, t, :], neg_s[:, t, :], ACT.Exp, bias=neg_max[:, t:t + 1],
                             scale=-1.0).then_inc(s["expd"], 1)

            def move_transposed(h, t):
                n = h * NT + t
                act.wait_ge(s["pt_mm"], n + 1)
                wait(act, "pv", n - 3)
                a.copy(prob_t[:, t, :], bank(2 + t % 2)).then_inc(s["pt_act"], 1)

            def head(h, first=False):
                for t in range(NT):
                    exponent(h, t)
                    if t == 1 and not first:
                        move_transposed(h - 1, 3)
                    if t == 3:
                        move_transposed(h, 1)

            head(0, True)
            head(1)
            with act.Fori(2, H) as h:
                head(h)
            move_transposed(H - 1, 3)

            for t in range(NT):
                act.wait_ge(s["oq_tp"], t + 1)
                a.copy(oq_t[:, t].rearrange("p k n -> p (k n)"), bank_bf(t % 2, CK * P)).then_inc(s["oq_t"], 1)
            act.wait_ge(s["var"], 2)
            a.activation(ln_std[:, 1, :], ln_var[:, 1, :], ACT.Sqrt).then_inc(s["std"], 1)
            for t in range(NT):
                at = slice(t * P, (t + 1) * P)
                act.wait_ge(s["xn_tp"], t + 1)
                src = bank(4 + t % 2, CK * P).rearrange("p (k n) -> p k n", k=CK)
                a.copy(xn_t[:, :, at], src)
                a.copy(xn_hi[:, :, at], src).then_inc(s["xn_hi"], 1)
            act.wait_ge(s["lg_sub"], 1)
            a.activation(r_e[:], r_e[:], ACT.Exp).then_inc(s["lg_exp"], 1)
            act.wait_ge(s["comb_tp"], 1)
            a.copy(comb_t[0:3 * E, :], bank(7, TOK, 3 * E)).then_inc(s["comb_sb"], 1)

            def silu_of(j, sl):
                act.wait_ge(s["g_mm"], j + 1)
                wait(act, "gated", j - 1)
                a.activation(silu[:, sl, :], bank(sl), ACT.Silu).then_inc(s["silu"], 1)

            def hidden_hi(j, sl):
                act.wait_ge(s["hid"], j + 1)
                wait(act, "dn_mm", j - 1)
                a.copy(hid_hi[:, sl, :], hid[:, sl, :]).then_inc(s["hid_hi"], 1)

            silu_of(0, 0)
            silu_of(1, 1)
            hidden_hi(0, 0)
            with act.Fori(1, FT // 2) as i:
                for sl in range(2):
                    silu_of(i * 2 + sl, sl)
                    hidden_hi(i * 2 + (sl - 1), 1 - sl)
            hidden_hi(FT - 1, 1)

        @block.vector
        def _(dve):
            v = nc.vector
            n = [0]

            def mark(ins):
                n[0] += 1
                ins.then_inc(s["dve_step"], 1)
                return n[0]

            def after(count):
                dve.wait_ge(s["dve_step"], count)

            def layer_norm(src, i):
                for t in range(NT):
                    if i:
                        after(ready[t])
                    c = mark(v.bn_stats(ln_stats[:, i, t, :], src[:, t, :]))
                after(c)
                for t in range(NT):
                    c = mark(v.bn_aggr(ln_mv[:, i, t, :], ln_stats[:, i, t, :]))
                after(c)
                v.tensor_scalar(ln_var[:, i, :], ln_mv[:, i, :, 1], LN_EPS, None, ALU.add).then_inc(s["var"], 1)
                dve.wait_ge(s["std"], i + 1)
                after(mark(v.reciprocal(ln_rstd[:, i, :], ln_std[:, i, :])))
                for t in range(NT):
                    v.tensor_scalar(xn[:, t, :], src[:, t, :], ln_mv[:, i, t, 0:1], ln_rstd[:, i, t:t + 1],
                                    ALU.subtract, ALU.mult).then_inc(s["xn2" if i else "xn1"], 1)

            def quantise(src, i, tiles, dst, done):
                after(mark(v.tensor_reduce(amax[:, i, 0:tiles], src, AX.X, ALU.max, apply_absolute_value=True)))
                after(mark(v.tensor_scalar(scale[:, i, 0:tiles], amax[:, i, 0:tiles], 1.0 / QMAX, Q_EPS, ALU.mult, ALU.max)))
                after(mark(v.reciprocal(rscale[:, i, 0:tiles], scale[:, i, 0:tiles])))
                c = [mark(v.tensor_scalar(src[:, t, :], src[:, t, :], rscale[:, i, t:t + 1], QMAX, ALU.mult, ALU.min))
                     for t in range(tiles)]
                for t in range(tiles):
                    after(c[t])
                    c[t] = mark(v.tensor_scalar(src[:, t, :], src[:, t, :], -QMAX, ROUND, ALU.max, ALU.add))
                for t in range(tiles):
                    after(c[t])
                    v.tensor_scalar(dst[:, t, :], src[:, t, :], ROUND, None, ALU.subtract).then_inc(s[done], 1)

            dve.wait_ge(s["wk_hi"], 1)
            v.tensor_tensor(wk_lo[:], twice(wk_sb[:].rearrange("p k c -> p (k c)")), fr(wk_hi[:]), ALU.subtract).then_inc(s["wk_lo"], 1)
            dve.wait_ge(ld["x"], 16)
            layer_norm(x_sb, 0)
            dve.wait_ge(s["xn1"], NT)
            quantise(xn[:], 0, NT, xq, "xq")
            dve.wait_ge(ld["wq"], 16)
            quantise(wq_sb[:], 1, CK, wqq, "wqq")
            dve.wait_ge(ld["wo"], 16)
            quantise(wo_sb[:], 2, CK, woq, "woq")
            dve.wait_ge(s["const_sel"], 1)
            v.tensor_scalar(expert_sel[:], expert_of[:], part_mod[:, 0:1], None, ALU.is_equal).then_inc(s["sel"], 1)

            dve.wait_ge(ld["bq"], 32)
            for i in range(G):
                f = q_f[:, i % 2, :]
                dve.wait_ge(s["q_mm"], i + 1)
                dve.wait_ge(s["qs_sb"], i + 1)
                v.tensor_tensor(f, bank(i % 2), q_scale[:, i % 2, :], ALU.mult).then_inc(s["q_acc_read"], 1)
                dve.wait_ge(s["q_acc_read"], i + 1)
                after(mark(v.tensor_scalar(f, f, bq_sb[:, i:i + 1], float(D) ** -0.5, ALU.add, ALU.mult)))
                after(mark(v.tensor_copy(q_hi[:, i * TOK:(i + 1) * TOK], f)))
                v.tensor_tensor(q_lo[:, i * TOK:(i + 1) * TOK], f, fr(q_hi[:, i * TOK:(i + 1) * TOK]), ALU.subtract).then_inc(s["q_done"], 1)

            dve.wait_ge(s["const_pad"], 1)
            dve.wait_ge(ld["bv"], 16)
            for i in range(B * LC):
                dve.wait_ge(s["v_mm"], i + 1)
                v.tensor_tensor(val[:, i // LC, i % LC, :, 0:D], bank(2 + i % 2, C).rearrange("p (h d) -> p h d", h=H),
                                bv_sb[:].rearrange("p (h d) -> p h d", h=H), ALU.add).then_inc(s["v_done"], 1)

            dve.wait_ge(ld["mask"], 16)

            def add_mask(h, t):
                n = h * NT + t
                dve.wait_ge(s["score"], n + 1)
                wait(dve, "expd", n - 3)
                dve.sem_inc(s["sm_turn"], 1)
                v.tensor_tensor_reduce(neg_s[:, t, :], bank(t % 2), mask_sb[:, t, :], -1.0, BIG, ALU.add, ALU.min,
                                       neg_max[:, t:t + 1]).then_inc(s["sm"], 1)

            def move_transposed(h, t):
                n = h * NT + t
                dve.wait_ge(s["pt_mm"], n + 1)
                wait(dve, "pv", n - 3)
                v.tensor_copy(prob_t[:, t, :], bank(2 + t % 2)).then_inc(s["pt_dve"], 1)

            def head(h, first=False):
                for t in range(NT):
                    add_mask(h, t)
                    if t == 0 and not first:
                        move_transposed(h - 1, 2)
                    if t == 2:
                        move_transposed(h, 0)

            head(0, True)
            head(1)
            with dve.Fori(2, H) as h:
                head(h)
            move_transposed(H - 1, 2)

            c = []
            for t in range(NT):
                dve.wait_ge(s["pv"], H * NT - NT + t + 1)
                acc = bank(4 + t, H * PV).rearrange("p (h d) -> p h d", h=H)
                c.append(mark(v.reciprocal(rsum[:, t, :], acc[:, :, D])))
            for t in range(NT):
                after(c[t])
                acc = bank(4 + t, H * PV).rearrange("p (h d) -> p h d", h=H)
                c[t] = mark(v.tensor_tensor(o_sb[:, t, :].rearrange("p (h d) -> p h d", h=H), acc[:, :, 0:D],
                                            rsum[:, t, :].unsqueeze(2).to_broadcast([P, H, D]), ALU.mult))
            after(c[-1])
            quantise(o_sb[:], 3, NT, oq, "oq")
            dve.wait_ge(s["wo_sc"], 1)
            dve.wait_ge(s["x_bo"], 1)
            ready = []
            for t in range(NT):
                dve.wait_ge(s["o_mm"], t + 1)
                v.scalar_tensor_tensor(proj[:, t, :], bank(2 + t % 2, C), scale[:, 3, t:t + 1], wo_scale[:],
                                       ALU.mult, ALU.mult).then_inc(s["o_read"], 1)
                dve.wait_ge(s["o_read"], t + 1)
                ready.append(mark(v.tensor_tensor(x2[:, t, :], proj[:, t, :], x_bo[:, t, :], ALU.add)))
            layer_norm(x2, 1)

            r = lambda ap: ap.unsqueeze(2)
            dve.wait_ge(s["lg_mm"], NT)
            lg = bank(6, NT * E).rearrange("p (t e) -> p t e", t=NT)
            after(mark(v.tensor_reduce(r_max[:], lg, AX.X, ALU.max)))
            v.tensor_tensor(r_e[:], lg, r(r_max[:]).to_broadcast([P, NT, E]), ALU.subtract).then_inc(s["lg_sub"], 1)
            dve.wait_ge(s["lg_exp"], 1)
            after(mark(v.tensor_reduce(r_sum[:, 0, :], r_e[:], AX.X, ALU.add)))
            after(mark(v.reciprocal(r_sum[:, 0, :], r_sum[:, 0, :])))
            dve.wait_ge(s["const_pad"], 2)
            after(mark(v.tensor_tensor(r_p[:, :, 0:E], r_e[:], r(r_sum[:, 0, :]).to_broadcast([P, NT, E]), ALU.mult)))
            for t in range(NT):
                c = mark(v.max(r_top[:, t, :], r_p[:, t, 0:E]))
            after(c)

            def inverse_sum(src, row):
                total = r_sum[:, row, :]
                after(mark(v.tensor_reduce(total, src, AX.X, ALU.add)))
                after(mark(v.tensor_scalar(total, total, 1e-12, None, ALU.max)))
                after(mark(v.reciprocal(total, total)))

            inverse_sum(r_top[:], 1)
            after(mark(v.tensor_tensor(r_ren[:], r_top[:], r(r_sum[:, 1, :]).to_broadcast([P, NT, TOPK]), ALU.mult)))
            for t in range(NT):
                c = mark(v.tensor_tensor_scan(r_cum[:, t, :], r_ren[:, t, :], r_zero[:], 0.0, ALU.add, ALU.add))
            after(c)
            after(mark(v.tensor_scalar(r_act[:, :, 1:TOPK], r_cum[:, :, 0:TOPK - 1], KEEP, None, ALU.is_lt)))
            after(mark(v.tensor_tensor(r_rw[:], r_top[:], r_act[:], ALU.mult)))
            after(mark(v.scalar_tensor_tensor(r_find[:], r_act[:], -1.0, r_rw[:], ALU.add, ALU.add)))
            for t in range(NT):
                mark(v.match_replace(r_rep[:, t, :], r_find[:, t, :], r_p[:, t, :], -2.0))
            inverse_sum(r_rw[:], 2)
            after(mark(v.scalar_tensor_tensor(comb[:], r_rep[:, :, 0:E], -1.5, r_p[:, :, 0:E], ALU.is_lt, ALU.mult)))
            for t in range(NT):
                v.tensor_scalar(comb3[:, t, :, :], comb[:, t, :].unsqueeze(1).to_broadcast([P, 3, E]),
                                r_sum[:, 2, t:t + 1], None, ALU.mult).then_inc(s["comb"], 1)
            dve.wait_ge(s["comb_sb"], 1)
            ct, cp = comb_t[0:3 * E, :], comb_part[0:3 * E, :]
            for a in range(2):
                after(mark(v.tensor_copy(cp, ct)))
                after(mark(v.scalar_tensor_tensor(ct, cp, part_step[0:3 * E, a:a + 1], ct, ALU.mult, ALU.add)))
            v.tensor_copy(cp, ct).then_inc(s["comb_part"], 1)

            def gate_up(j, sl):
                dve.wait_ge(s["u_mm"], j + 1)
                dve.wait_ge(s["silu"], j + 1)
                v.tensor_tensor(gated[:, sl, :], silu[:, sl, :], bank(2 + sl), ALU.mult).then_inc(s["gated"], 1)

            def weigh(j, sl):
                dve.wait_ge(s["gated"], j + 1)
                dve.wait_ge(s["ce_mm"], j + 1)
                wait(dve, "hid_hi", j - 1)
                v.tensor_tensor(hid[:, sl, :], gated[:, sl, :], bank(4 + sl), ALU.mult).then_inc(s["hid"], 1)

            def hidden_lo(j, sl):
                dve.wait_ge(s["hid_hi"], j + 1)
                wait(dve, "dn_mm", j - 1)
                v.tensor_tensor(hid_lo[:, sl, :], hid[:, sl, :], fr(hid_hi[:, sl, :]), ALU.subtract).then_inc(s["hid_lo"], 1)

            gate_up(0, 0)
            gate_up(1, 1)
            weigh(0, 0)
            hidden_lo(0, 0)
            with dve.Fori(1, FT // 2) as i:
                for sl in range(2):
                    gate_up(i * 2 + sl, sl)
                    weigh(i * 2 + (sl - 1), 1 - sl)
                    hidden_lo(i * 2 + (sl - 1), 1 - sl)
            weigh(FT - 1, 1)
            hidden_lo(FT - 1, 1)
            for t in range(NT):
                dve.wait_ge(s["y_mm"], t // 2 * 2 + 2)
                v.tensor_tensor(y_sb[:, t, :], ps[:, 6 + t // 2, (t % 2) * C:(t % 2 + 1) * C], x2[:, t, :],
                                ALU.add).then_inc(s["y_done"], 1)

        @block.tensor
        def _(pe):
            mm = nc.tensor.matmul

            def product(acc, terms):
                for i, (lhs, rhs) in enumerate(terms):
                    ins = mm(acc, lhs, rhs, start=(i == 0), stop=(i == len(terms) - 1))
                return ins

            def key_proj(i):
                gi, b = i // B, i % B
                wait(pe, "k_act", i - 1)
                pe.wait_ge(s["ctx_lo"], CK * (b + 1))
                at = slice(b * L, (b + 1) * L)
                product(bank(i % 2), [
                    (w[:, k * G + gi].rearrange("p a c -> p (a c)"), c[:, k, at])
                    for k in range(CK) for w, c in ((wk_hi, ctx_hi), (wk_hi, ctx_lo), (wk_lo, ctx_hi))
                ]).then_inc(s["k_mm"], 1)

            def transposes(dst, src, tiles):
                for t in range(tiles):
                    for k in range(CK):
                        ins = nc.tensor.transpose(dst[:, k, t * P:(t + 1) * P], src[:, t, k * P:(k + 1) * P], ident_bf[:])
                return ins

            pe.wait_ge(s["wk_lo"], 1)
            for i in range(5):
                key_proj(i)
            pe.wait_ge(s["const_ident"], 3)
            pe.wait_ge(s["xq"], NT)
            transposes(bank_bf(4, CK * TOK).rearrange("p (k n) -> p k n", k=CK), xq, NT).then_inc(s["xq_tp"], 1)
            pe.wait_ge(s["wqq"], CK)
            transposes(bank_bf(5, CK * C).rearrange("p (k n) -> p k n", k=CK), wqq, CK).then_inc(s["w_tp"], 1)
            pe.wait_ge(s["woq"], CK)
            for t in range(NT):
                nc.tensor.transpose(ps[0:1, 6, t * P:(t + 1) * P], scale[:, 0, t:t + 1], ident[:])
            for w in range(2):
                for k in range(CK):
                    ins = nc.tensor.transpose(ps[0:1, 7, w * C + k * P:w * C + (k + 1) * P], scale[:, 1 + w, k:k + 1], ident[:])
            ins.then_inc(s["row_tp"], 1)
            for i in range(5, G * B):
                key_proj(i)
            pe.wait_ge(s["xq_t"], 1)
            transposes(bank_bf(4, CK * C).rearrange("p (k n) -> p k n", k=CK), woq, CK).then_inc(s["w_tp"], 1)
            pe.wait_ge(s["rows"], 1)
            pe.wait_ge(s["wqq_t"], 1)
            for i in range(G):
                wait(pe, "qs_sb", i - 1)
                mm(bank(6 + i % 2), wq_scale_row[:, i].rearrange("p a c -> p (a c)"), x_scale_row[:], start=True, stop=True).then_inc(s["outer_mm"], 1)
                if i < 2:
                    pe.wait_ge(s["k_act"], G * B - 1 + i)
                wait(pe, "q_acc_read", i - 1)
                product(bank(i % 2), [(wqq_t[:, k * G + i].rearrange("p a c -> p (a c)"), xq_t[:, k, :]) for k in range(CK)]).then_inc(s["q_mm"], 1)
            mm(bank(5, C), ones_row[:], wo_scale_row[:], start=True, stop=True).then_inc(s["wo_sc_mm"], 1)
            pe.wait_ge(s["wv_lo"], 1)
            for i in range(B * LC):
                wait(pe, "v_done", i - 1)
                at = slice(i * P, (i + 1) * P)
                product(bank(2 + i % 2, C), [
                    (c[:, k, at], w[:, k, :])
                    for k in range(CK) for w, c in ((wv_hi, ctx_hi), (wv_lo, ctx_hi), (wv_hi, ctx_lo))
                ]).then_inc(s["v_mm"], 1)

            def scores(h, t):
                n = h * NT + t
                pe.wait_ge(s["qm"], h * (NT // 2) + (t // 2 + 1))
                wait(pe, "sm", n - 1)
                kb = key[:, group_at(h, B * L, t // NTB * L, L)]
                at = slice(t * P, (t + 1) * P)
                product(bank(t % 2), [(qm_hi[:, at], kb), (qm_lo[:, at], kb)]).then_inc(s["score"], 1)

            def prob_moved(h, t):
                pe.wait_ge(s["pt_act" if t % 2 else "pt_dve"], h * (NT // 2) + (t // 2 + 1))

            def transpose_probs(h, t):
                pe.wait_ge(s["expd"], h * NT + (t + 1))
                for k in range(LC):
                    at = slice(k * P, (k + 1) * P)
                    ins = nc.tensor.transpose(ps[:, 2 + t % 2, at], prob[:, t, at], ident[:])
                ins.then_inc(s["pt_mm"], 1)

            def values(h, t):
                o = ps[:, 4 + t, bass.ds(h * PV, PV)]
                product(o, [(prob_t[:, t, k * P:(k + 1) * P], val[:, t // NTB, k, bass.ds(h, 1), :].squeeze(1))
                            for k in range(LC)]).then_inc(s["pv"], 1)

            def head(h, start):
                for t in range(NT):
                    scores(h, t)
                    if not start:
                        prob_moved(h - 1, t)
                    if t >= 2:
                        transpose_probs(h, t - 2)
                    elif not start:
                        transpose_probs(h - 1, t + 2)
                    if not start:
                        values(h - 1, t)

            pe.wait_ge(s["q_acc_read"], G)
            pe.wait_ge(s["k_done"], G * B)
            pe.wait_ge(s["v_done"], B * LC)
            pe.wait_ge(s["qs_sb"], G)
            pe.wait_ge(s["woq_t"], 1)
            pe.wait_ge(s["wo_sc"], 1)
            head(0, True)
            with pe.Fori(1, H) as h:
                head(h, False)
            for t in range(NT):
                prob_moved(H - 1, t)
                if t < 2:
                    transpose_probs(H - 1, t + 2)
                values(H - 1, t)

            def out_proj(t):
                pe.wait_ge(s["oq_t"], t + 1)
                wait(pe, "o_read", t - 1)
                product(bank(2 + t % 2, C), [(oq_t[:, t, k, :], woq_t[:, k, :]) for k in range(CK)]).then_inc(s["o_mm"], 1)

            def logits(t):
                pe.wait_ge(s["xn_hi"], t + 1)
                for k in range(CK):
                    ins = mm(ps[:, 6, t * E:(t + 1) * E], xn_t[:, k, t * P:(t + 1) * P], gate_sb[:, k, :],
                             start=(k == 0), stop=(k == CK - 1))
                ins.then_inc(s["lg_mm"], 1)

            for t in range(NT):
                pe.wait_ge(s["oq"], t + 1)
                wait(pe, "oq_t", t - 1)
                tp = bank_bf(t % 2, CK * P).rearrange("p (k n) -> p k n", k=CK)
                for k in range(CK):
                    ins = nc.tensor.transpose(tp[:, k, :], oq[:, t, k * P:(k + 1) * P], ident_bf[:])
                ins.then_inc(s["oq_tp"], 1)
                if t:
                    out_proj(t - 1)
            out_proj(NT - 1)

            pe.wait_ge(ld["gate"], 16)
            for t in range(NT):
                pe.wait_ge(s["xn2"], t + 1)
                wait(pe, "xn_hi", t - 1)
                for k in range(CK):
                    ins = nc.tensor.transpose(ps[:, 4 + t % 2, k * P:(k + 1) * P], xn[:, t, k * P:(k + 1) * P], ident[:])
                ins.then_inc(s["xn_tp"], 1)
                if t:
                    logits(t - 1)
            logits(NT - 1)

            def gate_and_up(j, sl):
                pe.wait_ge(s["gu_split"], j + 1)
                for u, freed, done in ((0, "silu", "g_mm"), (1, "gated", "u_mm")):
                    wait(pe, freed, j - 1)
                    product(bank(2 * u + sl), [
                        (w[:, sl, (2 * k + u) * P:(2 * k + u + 1) * P], xt[:, k, :])
                        for k in range(CK) for w, xt in ((w_hi_gu, xn_hi), (w_lo_gu, xn_hi), (w_hi_gu, xn_lo))
                    ]).then_inc(s[done], 1)

            def token_weights(j, sl):
                wait(pe, "hid", j - 1)
                mm(bank(4 + sl), expert_sel[0:3 * E, bass.ds(j * P, P)], comb_part[0:3 * E, :], start=True, stop=True).then_inc(s["ce_mm"], 1)

            def down(j, sl, first=False, last=False):
                pe.wait_ge(s["hid_lo"], j + 1)
                pe.wait_ge(s["dn_split"], j + 1)
                for t in range(NT):
                    at = slice(t * P, (t + 1) * P)
                    acc = ps[:, 6 + t // 2, (t % 2) * C:(t % 2 + 1) * C]
                    terms = ((hid_hi, w_hi_dn), (hid_hi, w_lo_dn), (hid_lo, w_hi_dn))
                    for i, (hd, w) in enumerate(terms):
                        ins = mm(acc, hd[:, sl, at], w[:, sl, :], start=(first and i == 0 and t % 2 == 0),
                                 stop=(last and i == 2), skip_group_check=True)
                    if last:
                        ins.then_inc(s["y_mm"], 1)
                if not last:
                    ins.then_inc(s["dn_mm"], 1)

            pe.wait_ge(s["xn_lo"], NT)
            gate_and_up(0, 0)
            for t in range(NT):
                pe.wait_ge(s["comb"], t + 1)
                ins = nc.tensor.transpose(ps[0:3 * E, 7, t * P:(t + 1) * P], comb3[:, t].rearrange("p a e -> p (a e)"), ident[:])
            ins.then_inc(s["comb_tp"], 1)
            gate_and_up(1, 1)
            pe.wait_ge(s["comb_part"], 1)
            pe.wait_ge(s["sel"], 1)
            token_weights(0, 0)
            gate_and_up(2, 0)
            token_weights(1, 1)
            down(0, 0, first=True)
            gate_and_up(3, 1)
            token_weights(2, 0)
            down(1, 1)
            with pe.Fori(2, FT // 2) as i:
                for sl in range(2):
                    gate_and_up(i * 2 + sl, sl)
                    token_weights(i * 2 + (sl - 1), 1 - sl)
                    down(i * 2 + (sl - 2), sl)
            token_weights(FT - 1, 1)
            down(FT - 2, 0)
            down(FT - 1, 1, last=True)


def kernel(**inputs):
    import numpy as np
    import concourse.bacc as bacc
    from concourse.bass_utils import run_bass_kernel_spmd

    a = {k: np.asarray(v) for k, v in inputs.items()}
    gu = a["L0_ffn_gate_up_proj"].reshape(E, 2, INTER, CK, P)
    gu = gu.transpose(4, 3, 1, 0, 2).reshape(P, CK, 2, FT, P)
    arrays = {
        "x": a["x"].reshape(TOK, C),
        "ctx_t": a["ctx_2048"].reshape(B * L, C).T,
        "mask": a["mask_BxSxS2_ff0"],
        "wq": a["L0_xattn_wq"],
        "bq_t": a["L0_xattn_bq"].reshape(G, GC).T,
        "wk_t": a["L0_xattn_wk"].T,
        "bk_t": a["L0_xattn_bk"].reshape(G, GC).T,
        "wv_t": a["L0_xattn_wv"].T,
        "bv": a["L0_xattn_bv"],
        "wo": a["L0_xattn_wo"],
        "bo": a["L0_xattn_bo"],
        "gate_t": a["L0_ffn_gate_weight"].T,
        "gu_t": gu.transpose(0, 3, 1, 2, 4).reshape(P, FT, WGU),
        "down_t": a["L0_ffn_down_proj"].transpose(0, 2, 1).reshape(FT, P, C).transpose(1, 0, 2),
    }
    nc = bacc.Bacc("TRN2", target_bir_lowering=False, num_devices=1)
    arrays = {f"in_{k}": np.ascontiguousarray(v) for k, v in arrays.items()}
    args = [nc.dram_tensor(k, v.shape, mybir.dt.from_np(v.dtype), kind="ExternalInput").ap() for k, v in arrays.items()]
    out = nc.dram_tensor("out_0", (B, N, C), F32, kind="ExternalOutput").ap()
    build(nc, *args, out)
    return run_bass_kernel_spmd(nc, [arrays], core_ids=[0]).results[0]["out_0"]
```

```python
from contextlib import ExitStack

import concourse.bass as bass
from concourse import mybir

F32 = mybir.dt.float32
F32R = mybir.dt.float32r
BF16 = mybir.dt.bfloat16
ALU = mybir.AluOpType
ACT = mybir.ActivationFunctionType
AX = mybir.AxisListType

P = 128
B, N, L, C = 2, 256, 512, 256
H = 16
D = C // H
TOK = B * N
NT = TOK // P
NTB = N // P
CK = C // P
LC = L // P
HG = 4
G = H // HG
GC = HG * D
E, INTER, TOPK = 32, 96, 8
FT = E * INTER // P
WGU = CK * 2 * P
WRAW = WGU + C
PT_BANKS = (2, 3, 4, 6)
KEEP = 0.8
LN_EPS = 1e-5
Q_EPS = 1e-8
QMAX = 127.0
ROUND = 12582912.0
BIG = 3.0e38


def build(nc, x, ctx_t, mask, wq, bq_t, wk_t, bk_t, wv_t, bv, wo, bo, gate_t, gu_t, down_t, out):
    with ExitStack() as stack:
        def sem(name):
            return stack.enter_context(nc.semaphore(name))

        def sb_in(scope, name, shape, dt=F32):
            return scope.enter_context(nc.sbuf_tensor(name, shape, dt))

        def sb(name, shape, dt=F32):
            return sb_in(stack, name, shape, dt)

        ident = sb("ident", [P, P])
        ident_bf = sb("ident_bf", [P, P], BF16)
        ones_row = sb("ones_row", [1, P])
        hi_lo_sum = sb("hi_lo_sum", [P, GC])
        head_band = sb("head_band", [P, 2, H])
        head_mask = sb("head_mask", [P, H])
        part_col = sb("part_col", [P, 1])
        part_step = sb("part_step", [P, 2])
        part_mod = sb("part_mod", [P, 1])
        expert_sel = sb("expert_sel", [P, FT * P], BF16)
        x_sb = sb("x_sb", [P, NT, C])
        x_bo = x_sb
        x2 = x_sb
        xn = sb("xn", [P, NT, C])
        wo_sb = sb("wo_sb", [P, CK, C])
        woq = sb("woq", [P, CK, C], BF16)
        woq_t = sb("woq_t", [P, CK, C], BF16)
        wo_scale = sb("wo_scale", [P, C])
        gate_sb = sb("gate_sb", [P, CK, E])
        bq_sb = sb("bq_sb", [P, G])
        bk_sb = sb("bk_sb", [P, G])
        bo_sb = sb("bo_sb", [P, C])
        ln_stats = sb("ln_stats", [P, 2, NT, 6])
        ln_mv = sb("ln_mv", [P, 2, NT, 2])
        ln_var = sb("ln_var", [P, 2, NT])
        ln_std = sb("ln_std", [P, 2, NT])
        ln_rstd = sb("ln_rstd", [P, 2, NT])
        amax = sb("amax", [P, 4, NT])
        scale = sb("scale", [P, 4, NT])
        rscale = sb("rscale", [P, 4, NT])
        neg_max = sb("neg_max", [P, NT])
        p_sum = sb("p_sum", [P, NT, H])
        o_sb = sb("o_sb", [P, NT, C])
        ot_sb = sb("ot_sb", [P, TOK])
        r_max = sb("r_max", [P, NT])
        r_sum = sb("r_sum", [P, 3, NT])
        r_p = sb("r_p", [P, NT, E + TOPK])
        r_act = sb("r_act", [P, NT, TOPK])
        r_zero = sb("r_zero", [P, TOPK])

        first = ExitStack()

        def sb(name, shape, dt=F32):
            return sb_in(first, name, shape, dt)

        expert_of = sb("expert_of", [P, FT * P], BF16)
        ctx_sb = sb("ctx_sb", [P, CK, B * L])
        ctx_hi = sb("ctx_hi", [P, CK, B * L], F32R)
        ctx_lo = sb("ctx_lo", [P, CK, B * L], F32R)
        wq_sb = sb("wq_sb", [P, CK, C])
        wk_sb = sb("wk_sb", [P, CK, C])
        wk_hi = sb("wk_hi", [P, CK * G, 2, GC], F32R)
        wk_lo = sb("wk_lo", [P, CK * G, 2, GC], F32R)
        wv_sb = sb("wv_sb", [P, CK, C])
        wv_hi = sb("wv_hi", [P, CK, C], F32R)
        wv_lo = sb("wv_lo", [P, CK, C], F32R)
        bv_sb = sb("bv_sb", [P, C])
        key_f = sb("key_f", [P, 2, L])
        xq = sb("xq", [P, NT, C], BF16)
        xq_t = sb("xq_t", [P, CK, TOK], BF16)
        wqq = sb("wqq", [P, CK, C], BF16)
        wqq_t = sb("wqq_t", [P, CK * G, 2, GC], BF16)
        x_scale_row = sb("x_scale_row", [1, TOK])
        wq_scale_row = sb("wq_scale_row", [1, G, 2, GC])
        wo_scale_row = sb("wo_scale_row", [1, C])
        first.close()

        w_raw_gu = sb_in(stack, "w_raw_gu", [P, FT, WGU])

        second = ExitStack()

        def sb(name, shape, dt=F32):
            return sb_in(second, name, shape, dt)

        prob = sb("prob", [P, NT, L])
        pt_hi = sb("pt_hi", [P, B, LC, N], F32R)
        pt_lo = sb("pt_lo", [P, B, LC, N], F32R)
        mask_sb = sb("mask_sb", [P, NT, L])
        key = sb("key", [P, G * B * L], F32R)
        val = sb("val", [P, B * LC, H, D])
        val_head = sb("val_head", [P, HG, B * LC, HG * 2 * D], F32R)
        q_hi = sb("q_hi", [P, G * TOK], F32R)
        q_lo = sb("q_lo", [P, G * TOK], F32R)
        qm_hi = sb("qm_hi", [P, TOK], F32R)
        qm_lo = sb("qm_lo", [P, TOK], F32R)
        neg_s = sb("neg_s", [P, NT, L])
        second.close()
        q_scale, q_f = neg_s[:, 0:2, :], neg_s[:, 2:4, :]

        def sb(name, shape, dt=F32):
            return sb_in(stack, name, shape, dt)

        w_raw_dn = sb("w_raw_dn", [P, FT, C])
        oq = sb("oq", [P, NT, C], BF16)
        oq_t = sb("oq_t", [P, NT, CK, P], BF16)
        proj = sb("proj", [P, NT, C])
        xn_t = sb("xn_t", [P, CK, TOK])
        xn_hi = sb("xn_hi", [P, CK, TOK], F32R)
        xn_lo = sb("xn_lo", [P, CK, TOK], F32R)
        r_e = sb("r_e", [P, NT, E])
        r_top = sb("r_top", [P, NT, TOPK])
        r_ren = sb("r_ren", [P, NT, TOPK])
        r_cum = sb("r_cum", [P, NT, TOPK])
        r_rw = sb("r_rw", [P, NT, TOPK])
        r_find = sb("r_find", [P, NT, TOPK])
        r_rep = sb("r_rep", [P, NT, E + TOPK])
        comb = sb("comb", [P, NT, E])
        comb3 = sb("comb3", [P, NT, 3, E])
        comb_t = sb("comb_t", [P, TOK])
        comb_part = sb("comb_part", [P, TOK], BF16)
        w_hi_gu = sb("w_hi_gu", [P, 2, WGU], F32R)
        w_lo_gu = sb("w_lo_gu", [P, 2, WGU], F32R)
        w_hi_dn = sb("w_hi_dn", [P, 2, C], F32R)
        w_lo_dn = sb("w_lo_dn", [P, 2, C], F32R)
        silu = sb("silu", [P, 2, TOK])
        gated = sb("gated", [P, 2, TOK])
        hid = sb("hid", [P, 2, TOK])
        hid_hi = sb("hid_hi", [P, 2, TOK], F32R)
        hid_lo = sb("hid_lo", [P, 2, TOK], F32R)
        y_sb = sb("y_sb", [P, NT, C])

        ps = stack.enter_context(nc.psum_tensor("ps", [P, 8, 512], F32))

        def bank(i, n=512, rows=P):
            return ps[0:rows, i, 0:n]

        def bank_bf(i, n):
            return ps[:, i, 0:n // 2].bitcast(BF16)

        loads = ["x", "ctx0", "ctx1", "mask", "wq", "wo", "wk", "wv", "bq", "bk", "bv", "bo", "gate"]
        ld = {n: sem("ld_" + n) for n in loads}
        NGU = 4
        ld_gu = [sem(f"ld_gu{i}") for i in range(NGU)]
        ld_dn = sem("ld_dn")
        names = """ce_mm comb comb_part comb_sb comb_tp const_ident const_mask const_pad const_sel
            ctx_hi ctx_lo dn_hi dn_mm dn_split dve_step expd g_mm gated gu_hi gu_split hid hid_hi hid_lo
            k_act k_done k_mm lg_exp lg_mm lg_sub o_mm o_read oq oq_t oq_tp outer_mm
            pool_step ot out_got out_tp pt_hi pt_lo pt_mm pv v_hi v_split q_acc_read q_done q_mm qm qs_sb row_tp rows score
            sel silu sm sm_turn pool_turn std stored u_mm v_done v_mm var w_tp wk_hi wk_lo wo_sc wo_sc_mm woq
            woq_t wqq wqq_t wv_hi wv_lo x_bo xn1 xn2 xn_hi xn_lo xn_tp xq xq_t xq_tp y_done y_mm""".split()
        s = {n: sem("s_" + n) for n in names}

        block = stack.enter_context(nc.Block())

        def twice(ap):
            ap = ap.rearrange("p (g c) -> p g c", c=GC)
            return ap.unsqueeze(2).to_broadcast([ap.shape[0], ap.shape[1], 2, GC])

        def group_at(h, width, start, n):
            return bass.ds((h & (H - HG)) * (width // HG) + start, n)

        def at_head(h):
            return bass.ds(h, 1)

        def pt_bank(t):
            return bank(PT_BANKS[t]).rearrange("p (k n) -> p k n", k=LC)

        def pt_cols(buf, t):
            return buf[:, t // NTB, :, (t % NTB) * P:(t % NTB + 1) * P]

        def fr(ap):
            return ap.bitcast(F32)

        def wait(eng, name, count):
            if not isinstance(count, int) or count > 0:
                eng.wait_ge(s[name], count)

        x_dram = x.rearrange("(t p) c -> p t c", p=P)
        ctx_dram = ctx_t.rearrange("(k p) n -> p k n", p=P)
        out_dram = out.rearrange("b (t p) c -> p (b t) c", p=P)

        @block.sync
        def _(sp):
            sp.dma_start(x_sb[:], x_dram).then_inc(ld["x"], 16)
            sp.dma_start(ctx_sb[:, :, 0:L], ctx_dram[:, :, 0:L]).then_inc(ld["ctx0"], 16)
            sp.dma_start(wv_sb[:], wv_t.rearrange("(k p) n -> p k n", p=P)).then_inc(ld["wv"], 16)
            sp.dma_start(bv_sb[:], bv.partition_broadcast(P)).then_inc(ld["bv"], 16)
            sp.dma_start(mask_sb[:], mask.rearrange("b (t p) l -> p (b t) l", p=P)).then_inc(ld["mask"], 16)
            sp.wait_ge(s["v_done"], B * LC)
            sp.wait_ge(s["k_done"], G * B)
            sp.wait_ge(s["q_done"], G)
            for i in range(NGU):
                cut = slice(i * FT // NGU, (i + 1) * FT // NGU)
                sp.dma_start(w_raw_gu[:, cut, :], gu_t[:, cut, :]).then_inc(ld_gu[i], 16)
            sp.wait_ge(s["pv"], H * B)
            sp.dma_start(w_raw_dn[:], down_t).then_inc(ld_dn, 16)
            for t in range(NT):
                sp.wait_ge(s["y_done"], t + 1)
                sp.dma_start(out_dram[:, t, :], y_sb[:, t, :]).then_inc(s["stored"], 16)
            sp.wait_ge(s["stored"], 16 * NT)

        @block.gpsimd
        def _(pool):
            g = nc.gpsimd
            n = [0]

            def step(ins):
                n[0] += 1
                ins.then_inc(s["pool_step"], 1)
                pool.wait_ge(s["pool_step"], n[0])

            step(g.memset(ident[:], 0.0))
            g.affine_select(out=ident[:], in_=ident[:], compare_op=ALU.not_equal, fill=1.0, base=0,
                            pattern=[[-1, P]], channel_multiplier=1).then_inc(s["const_ident"], 1)
            pool.wait_ge(s["const_ident"], 1)
            g.tensor_copy(ident_bf[:], ident[:]).then_inc(s["const_ident"], 1)
            eye = ident[:].rearrange("p (h a d) -> p h a d", h=HG, a=2)
            g.tensor_tensor(hi_lo_sum[:].rearrange("p (h d) -> p h d", h=HG), eye[:, :, 0, :], eye[:, :, 1, :], ALU.add)
            g.memset(ones_row[:], 1.0).then_inc(s["const_ident"], 1)
            g.iota(expert_of[:], pattern=[[1, E], [0, INTER]], base=0, channel_multiplier=0,
                   allow_small_or_imprecise_dtypes=True)
            step(g.iota(part_col[:], pattern=[[0, 1]], base=0, channel_multiplier=1,
                        allow_small_or_imprecise_dtypes=True))
            step(g.tensor_scalar(part_mod[:], part_col[:], 32.0, -32.0, ALU.is_ge, ALU.mult))
            step(g.tensor_tensor(part_mod[:], part_mod[:], part_col[:], ALU.add))
            step(g.tensor_scalar(part_step[:, 1:2], part_col[:], 64.0, -32.0, ALU.is_ge, ALU.mult))
            step(g.tensor_tensor(part_mod[:], part_mod[:], part_step[:, 1:2], ALU.add))
            g.tensor_scalar(part_step[:, 0:1], part_col[:], 32.0, -1.0, ALU.is_ge, ALU.mult)
            g.tensor_scalar(part_step[:, 1:2], part_col[:], 64.0, -1.0, ALU.is_ge, ALU.mult).then_inc(s["const_sel"], 1)
            g.memset(fr(val_head[:]), 0.0).then_inc(s["const_pad"], 1)

            def low(lo, full, hi, done):
                g.tensor_tensor(lo, full, fr(hi), ALU.subtract).then_inc(s[done], 1)

            for b in range(B):
                for k in range(CK):
                    pool.wait_ge(s["ctx_hi"], b + 1)
                    at = slice(b * L, (b + 1) * L)
                    low(ctx_lo[:, k, at], ctx_sb[:, k, at], ctx_hi[:, k, at], "ctx_lo")

            step(g.memset(head_band[:], 1.0))
            band = head_band[:].rearrange("p d (a h) -> p d a h", h=HG)
            step(g.affine_select(out=band, in_=band, compare_op=ALU.is_ge, fill=0.0, base=0,
                                 pattern=[[-GC, 2], [0, G], [-D, HG]], channel_multiplier=1))
            step(g.affine_select(out=band, in_=band, compare_op=ALU.is_ge, fill=0.0, base=D - 1,
                                 pattern=[[GC, 2], [0, G], [D, HG]], channel_multiplier=-1))
            g.tensor_tensor(head_mask[:], head_band[:, 0, :], head_band[:, 1, :], ALU.add).then_inc(s["const_mask"], 1)
            g.memset(r_zero[:], 0.0)
            g.memset(r_act[:], 1.0)
            g.memset(r_p[:], -1.0).then_inc(s["const_pad"], 1)

            pool.wait_ge(s["const_pad"], 2)
            for i in range(G * B):
                if i == 1:
                    pool.wait_ge(s["k_done"], 1)
                    pool.wait_ge(s["wv_hi"], 1)
                    low(wv_lo[:], wv_sb[:], wv_hi[:], "wv_lo")
                    pool.wait_ge(s["wv_lo"], 1)
                pool.wait_ge(s["k_act"], i + 1)
                lo_rows = key[GC:P, i * L:(i + 1) * L]
                g.tensor_tensor(lo_rows, key_f[GC:P, i % 2, :], fr(lo_rows), ALU.subtract).then_inc(s["k_done"], 1)
            pool.wait_ge(s["k_done"], G * B)

            pool.wait_ge(s["const_mask"], 1)
            pool.wait_ge(s["q_done"], G)

            def mask_query(h, m):
                wait(pool, "score", h * NT + (2 * m + 2 - NT))
                pool.sem_inc(s["pool_turn"], 1)
                pool.sem_inc(s["pool_turn"], 1)
                cols = slice(m * 2 * P, (m + 1) * 2 * P)
                hm = head_mask[:, bass.ds(h, 1)].to_broadcast([P, 2 * P])
                for qm, q in ((qm_hi, q_hi), (qm_lo, q_lo)):
                    ins = g.tensor_tensor(qm[:, cols], fr(q[:, group_at(h, TOK, m * 2 * P, 2 * P)]), hm, ALU.mult)
                ins.then_inc(s["qm"], 1)

            for m in range(NT // 2):
                mask_query(0, m)
            pool.wait_ge(ld["x"], 16)
            pool.wait_ge(ld["bo"], 16)
            g.tensor_tensor(x_bo[:], x_sb[:], bo_sb[:].unsqueeze(1).to_broadcast([P, NT, C]), ALU.add).then_inc(s["x_bo"], 1)

            def split_values(h, hh):
                wait(pool, "pv", h * B + (B - HG * B))
                wait(pool, "v_hi", h + (1 - HG))
                pool.sem_inc(s["pool_turn"], 1)
                v = val[:, :, bass.ds(h, 1), :].squeeze(2)
                lo = (hh * 2 + 1) * D
                hi_cols = val_head[:, hh, :, lo - D:lo]
                g.tensor_copy(hi_cols, v).then_inc(s["v_hi"], 1)
                pool.wait_ge(s["v_hi"], h + 1)
                pool.sem_inc(s["pool_turn"], 1)
                g.tensor_tensor(val_head[:, hh, :, lo:lo + D], v, fr(hi_cols), ALU.subtract).then_inc(s["v_split"], 1)

            pool.wait_ge(s["v_done"], B * LC)
            split_values(0, 0)
            for hh in range(1, HG):
                for m in range(NT // 2):
                    mask_query(hh, m)
                split_values(hh, hh)
            with pool.Fori(1, G) as gr:
                for hh in range(HG):
                    for m in range(NT // 2):
                        mask_query(gr * HG + hh, m)
                    split_values(gr * HG + hh, hh)

            def lo_gu(j, sl):
                pool.wait_ge(s["gu_hi"], j + 1)
                pool.sem_inc(s["pool_turn"], 1)
                low(w_lo_gu[:, sl, :], w_raw_gu[:, bass.ds(j, 1), :].squeeze(1), w_hi_gu[:, sl, :], "gu_split")

            def lo_dn(j, sl):
                pool.wait_ge(s["dn_hi"], j + 1)
                pool.sem_inc(s["pool_turn"], 1)
                low(w_lo_dn[:, sl, :], w_raw_dn[:, bass.ds(j, 1), :].squeeze(1), w_hi_dn[:, sl, :], "dn_split")

            lo_gu(0, 0)
            for t in range(NT):
                pool.wait_ge(s["xn_hi"], t + 1)
                at = slice(t * P, (t + 1) * P)
                low(xn_lo[:, :, at], xn_t[:, :, at], xn_hi[:, :, at], "xn_lo")
            lo_gu(1, 1)
            lo_dn(0, 0)
            with pool.Fori(1, FT // 2) as i:
                for sl in range(2):
                    lo_gu(i * 2 + sl, sl)
                    lo_dn(i * 2 + (sl - 1), 1 - sl)
            lo_dn(FT - 1, 1)

        @block.scalar
        def _(act):
            a = nc.scalar
            dram = lambda w: w.rearrange("(k p) n -> p k n", p=P)
            act.dma_start(wk_sb[:], dram(wk_t)).then_inc(ld["wk"], 16)
            act.dma_start(wq_sb[:], dram(wq)).then_inc(ld["wq"], 16)
            act.dma_start(ctx_sb[:, :, L:2 * L], ctx_dram[:, :, L:2 * L]).then_inc(ld["ctx1"], 16)
            for half in range(2):
                act.dma_start(bk_sb[half * GC:(half + 1) * GC, :], bk_t).then_inc(ld["bk"], 16)
                act.dma_start(bq_sb[half * GC:(half + 1) * GC, :], bq_t).then_inc(ld["bq"], 16)
            act.dma_start(wo_sb[:], dram(wo)).then_inc(ld["wo"], 16)
            act.dma_start(bo_sb[:], bo.partition_broadcast(P)).then_inc(ld["bo"], 16)
            act.dma_start(gate_sb[:], dram(gate_t)).then_inc(ld["gate"], 16)

            act.wait_ge(ld["wk"], 16)
            a.copy(wk_hi[:], twice(wk_sb[:].rearrange("p k c -> p (k c)"))).then_inc(s["wk_hi"], 1)
            act.wait_ge(ld["ctx0"], 16)
            a.copy(ctx_hi[:, :, 0:L], ctx_sb[:, :, 0:L]).then_inc(s["ctx_hi"], 1)
            act.wait_ge(ld["ctx1"], 16)
            a.copy(ctx_hi[:, :, L:2 * L], ctx_sb[:, :, L:2 * L]).then_inc(s["ctx_hi"], 1)
            act.wait_ge(s["var"], 1)
            a.activation(ln_std[:, 0, :], ln_var[:, 0, :], ACT.Sqrt).then_inc(s["std"], 1)
            act.wait_ge(ld["wv"], 16)
            a.copy(wv_hi[:], wv_sb[:]).then_inc(s["wv_hi"], 1)

            act.wait_ge(ld["bk"], 32)

            def key_out(i):
                act.wait_ge(s["k_mm"], i + 1)
                gi = i // B
                a.activation(key[:, i * L:(i + 1) * L], bank(i % 2), ACT.Identity, bias=bk_sb[:, gi:gi + 1])
                if i >= 2:
                    act.wait_ge(s["k_done"], i - 1)
                a.activation(key_f[GC:P, i % 2, :], ps[GC:P, i % 2, :], ACT.Identity,
                             bias=bk_sb[GC:P, gi:gi + 1]).then_inc(s["k_act"], 1)

            for i in range(5):
                key_out(i)
            act.wait_ge(s["xq_tp"], 1)
            a.copy(xq_t[:].rearrange("p k n -> p (k n)"), bank_bf(4, CK * TOK)).then_inc(s["xq_t"], 1)
            act.wait_ge(s["w_tp"], 1)
            a.copy(wqq_t[:], twice(bank_bf(5, CK * C))).then_inc(s["wqq_t"], 1)
            act.wait_ge(s["row_tp"], 1)
            a.copy(x_scale_row[:], bank(6, TOK, 1))
            a.copy(wq_scale_row[:], twice(bank(7, C, 1)))
            a.copy(wo_scale_row[:], ps[0:1, 7, C:2 * C]).then_inc(s["rows"], 1)
            for i in range(5, G * B):
                key_out(i)
            act.wait_ge(s["w_tp"], 2)
            a.copy(woq_t[:].rearrange("p k n -> p (k n)"), bank_bf(4, CK * C)).then_inc(s["woq_t"], 1)
            for i in range(G):
                act.wait_ge(s["outer_mm"], i + 1)
                if i >= 2:
                    act.wait_ge(s["q_acc_read"], i - 1)
                a.copy(q_scale[:, i % 2, :], bank(6 + i % 2)).then_inc(s["qs_sb"], 1)
            act.wait_ge(s["wo_sc_mm"], 1)
            a.copy(wo_scale[:], bank(5, C)).then_inc(s["wo_sc"], 1)

            def exponent(h, t):
                n = h * NT + t
                act.wait_ge(s["sm"], n + 1)
                wait(act, "pt_mm", n - 3)
                a.activation(prob[:, t, :], neg_s[:, t, :], ACT.Exp, bias=neg_max[:, t:t + 1],
                             scale=-1.0, accum_out=p_sum[:, t, at_head(h)]).then_inc(s["expd"], 1)

            def transposed_hi(h, t):
                n = h * NT + t
                act.wait_ge(s["pt_mm"], n + 1)
                wait(act, "pv", h * B + (t // NTB - 1))
                a.copy(pt_cols(pt_hi, t), pt_bank(t)).then_inc(s["pt_hi"], 1)

            def move_out(gr):
                act.wait_ge(s["pv"], gr * (HG * B) + HG * B)
                a.copy(ot_sb[:], bank(5)).then_inc(s["ot"], 1)

            def group(gr, first=False):
                for hh in range(HG):
                    h = gr * HG + hh
                    for t in range(NT):
                        exponent(h, t)
                        if t >= 2:
                            transposed_hi(h, t - 2)
                        elif not (first and hh == 0):
                            transposed_hi(h - 1, t + 2)
                        if hh == 1 and t == 0 and not first:
                            move_out(gr - 1)

            group(0, True)
            with act.Fori(1, G) as gr:
                group(gr)
            for t in (2, 3):
                transposed_hi(H - 1, t)
            move_out(G - 1)

            def hi_gu(j, sl):
                wait(act, "u_mm", j - 1)
                a.copy(w_hi_gu[:, sl, :], w_raw_gu[:, bass.ds(j, 1), :].squeeze(1)).then_inc(s["gu_hi"], 1)

            def hi_dn(j, sl):
                wait(act, "dn_mm", j - 1)
                a.copy(w_hi_dn[:, sl, :], w_raw_dn[:, bass.ds(j, 1), :].squeeze(1)).then_inc(s["dn_hi"], 1)

            act.wait_ge(s["pv"], H * B)
            for q in (*ld_gu, ld_dn):
                act.wait_ge(q, 16)
            hi_gu(0, 0)

            for t in range(NT):
                act.wait_ge(s["oq_tp"], t + 1)
                a.copy(oq_t[:, t].rearrange("p k n -> p (k n)"), bank_bf(t % 2, CK * P)).then_inc(s["oq_t"], 1)
            act.wait_ge(s["var"], 2)
            a.activation(ln_std[:, 1, :], ln_var[:, 1, :], ACT.Sqrt).then_inc(s["std"], 1)
            for t in range(NT):
                at = slice(t * P, (t + 1) * P)
                act.wait_ge(s["xn_tp"], t + 1)
                src = bank(4 + t % 2, CK * P).rearrange("p (k n) -> p k n", k=CK)
                a.copy(xn_t[:, :, at], src)
                a.copy(xn_hi[:, :, at], src).then_inc(s["xn_hi"], 1)
            hi_gu(1, 1)
            act.wait_ge(s["lg_sub"], 1)
            a.activation(r_e[:], r_e[:], ACT.Exp).then_inc(s["lg_exp"], 1)
            act.wait_ge(s["comb_tp"], 1)
            a.copy(comb_t[0:3 * E, :], bank(7, TOK, 3 * E)).then_inc(s["comb_sb"], 1)

            def silu_of(j, sl):
                act.wait_ge(s["g_mm"], j + 1)
                wait(act, "gated", j - 1)
                a.activation(silu[:, sl, :], bank(sl), ACT.Silu).then_inc(s["silu"], 1)

            def hidden_hi(j, sl):
                act.wait_ge(s["hid"], j + 1)
                wait(act, "dn_mm", j - 1)
                a.copy(hid_hi[:, sl, :], hid[:, sl, :]).then_inc(s["hid_hi"], 1)

            def expert_step(j, sl, last=False):
                if not last:
                    hi_gu(j + 1, 1 - sl)
                hi_dn(j - 1, 1 - sl)
                silu_of(j, sl)
                hidden_hi(j - 1, 1 - sl)

            silu_of(0, 0)
            expert_step(1, 1)
            with act.Fori(1, FT // 2 - 1) as i:
                for sl in range(2):
                    expert_step(i * 2 + sl, sl)
            expert_step(FT - 2, 0)
            expert_step(FT - 1, 1, last=True)
            hi_dn(FT - 1, 1)
            hidden_hi(FT - 1, 1)

        @block.vector
        def _(dve):
            v = nc.vector
            n = [0]

            def mark(ins):
                n[0] += 1
                ins.then_inc(s["dve_step"], 1)
                return n[0]

            def after(count):
                dve.wait_ge(s["dve_step"], count)

            def layer_norm(src, i):
                for t in range(NT):
                    if i:
                        after(ready[t])
                    c = mark(v.bn_stats(ln_stats[:, i, t, :], src[:, t, :]))
                after(c)
                for t in range(NT):
                    c = mark(v.bn_aggr(ln_mv[:, i, t, :], ln_stats[:, i, t, :]))
                after(c)
                v.tensor_scalar(ln_var[:, i, :], ln_mv[:, i, :, 1], LN_EPS, None, ALU.add).then_inc(s["var"], 1)
                dve.wait_ge(s["std"], i + 1)
                after(mark(v.reciprocal(ln_rstd[:, i, :], ln_std[:, i, :])))
                for t in range(NT):
                    v.tensor_scalar(xn[:, t, :], src[:, t, :], ln_mv[:, i, t, 0:1], ln_rstd[:, i, t:t + 1],
                                    ALU.subtract, ALU.mult).then_inc(s["xn2" if i else "xn1"], 1)

            def quantise(src, i, tiles, dst, done):
                after(mark(v.tensor_reduce(amax[:, i, 0:tiles], src, AX.X, ALU.max, apply_absolute_value=True)))
                after(mark(v.tensor_scalar(scale[:, i, 0:tiles], amax[:, i, 0:tiles], 1.0 / QMAX, Q_EPS, ALU.mult, ALU.max)))
                after(mark(v.reciprocal(rscale[:, i, 0:tiles], scale[:, i, 0:tiles])))
                c = [mark(v.tensor_scalar(src[:, t, :], src[:, t, :], rscale[:, i, t:t + 1], QMAX, ALU.mult, ALU.min))
                     for t in range(tiles)]
                for t in range(tiles):
                    after(c[t])
                    c[t] = mark(v.tensor_scalar(src[:, t, :], src[:, t, :], -QMAX, ROUND, ALU.max, ALU.add))
                for t in range(tiles):
                    after(c[t])
                    v.tensor_scalar(dst[:, t, :], src[:, t, :], ROUND, None, ALU.subtract).then_inc(s[done], 1)

            dve.wait_ge(s["wk_hi"], 1)
            v.tensor_tensor(wk_lo[:], twice(wk_sb[:].rearrange("p k c -> p (k c)")), fr(wk_hi[:]), ALU.subtract).then_inc(s["wk_lo"], 1)
            dve.wait_ge(ld["x"], 16)
            layer_norm(x_sb, 0)
            dve.wait_ge(s["xn1"], NT)
            quantise(xn[:], 0, NT, xq, "xq")
            dve.wait_ge(ld["wq"], 16)
            quantise(wq_sb[:], 1, CK, wqq, "wqq")
            dve.wait_ge(ld["wo"], 16)
            quantise(wo_sb[:], 2, CK, woq, "woq")
            dve.wait_ge(s["const_sel"], 1)
            v.tensor_scalar(expert_sel[:], expert_of[:], part_mod[:, 0:1], None, ALU.is_equal).then_inc(s["sel"], 1)

            dve.wait_ge(ld["bq"], 32)
            for i in range(G):
                f = q_f[:, i % 2, :]
                dve.wait_ge(s["q_mm"], i + 1)
                dve.wait_ge(s["qs_sb"], i + 1)
                v.tensor_tensor(f, bank(i % 2), q_scale[:, i % 2, :], ALU.mult).then_inc(s["q_acc_read"], 1)
                dve.wait_ge(s["q_acc_read"], i + 1)
                after(mark(v.tensor_scalar(f, f, bq_sb[:, i:i + 1], float(D) ** -0.5, ALU.add, ALU.mult)))
                after(mark(v.tensor_copy(q_hi[:, i * TOK:(i + 1) * TOK], f)))
                v.tensor_tensor(q_lo[:, i * TOK:(i + 1) * TOK], f, fr(q_hi[:, i * TOK:(i + 1) * TOK]), ALU.subtract).then_inc(s["q_done"], 1)

            dve.wait_ge(ld["bv"], 16)
            for i in range(B * LC):
                dve.wait_ge(s["v_mm"], i + 1)
                v.tensor_tensor(val[:, i], bank(2 + i % 2, C).rearrange("p (h d) -> p h d", h=H),
                                bv_sb[:].rearrange("p (h d) -> p h d", h=H), ALU.add).then_inc(s["v_done"], 1)

            dve.wait_ge(ld["mask"], 16)

            def add_mask(h, t):
                n = h * NT + t
                dve.wait_ge(s["score"], n + 1)
                wait(dve, "expd", n - 3)
                dve.sem_inc(s["sm_turn"], 1)
                v.tensor_tensor_reduce(neg_s[:, t, :], bank(t % 2), mask_sb[:, t, :], -1.0, BIG, ALU.add, ALU.min,
                                       neg_max[:, t:t + 1]).then_inc(s["sm"], 1)

            def transposed_lo(h, t):
                n = h * NT + t
                dve.wait_ge(s["pt_hi"], n + 1)
                hi = pt_cols(pt_hi, t)
                v.tensor_tensor(pt_cols(pt_lo, t), pt_bank(t), fr(hi), ALU.subtract).then_inc(s["pt_lo"], 1)

            def gather_out(gr):
                dve.wait_ge(s["out_tp"], gr + 1)
                v.tensor_copy(o_sb[:, :, bass.ds(gr * GC, GC)], bank(7, NT * GC).rearrange("p (t c) -> p t c", t=NT)).then_inc(s["out_got"], 1)

            def group(gr, first=False):
                for hh in range(HG):
                    h = gr * HG + hh
                    for t in range(NT):
                        add_mask(h, t)
                        if t == 3:
                            transposed_lo(h, 0)
                        elif not (first and hh == 0):
                            transposed_lo(h - 1, t + 1)
                        if hh == 1 and t == 3 and not first:
                            gather_out(gr - 1)

            dve.sem_inc(s["out_got"], 1)
            group(0, True)
            with dve.Fori(1, G) as gr:
                group(gr)
            for t in (1, 2, 3):
                transposed_lo(H - 1, t)
            gather_out(G - 1)

            dve.wait_ge(s["expd"], H * NT)
            dve.wait_ge(s["out_got"], G + 1)
            after(mark(v.reciprocal(p_sum[:], p_sum[:])))
            o4 = o_sb[:].rearrange("p t (h d) -> p t h d", d=D)
            after(mark(v.tensor_tensor(o4, o4, p_sum[:].unsqueeze(3).to_broadcast([P, NT, H, D]), ALU.mult)))
            quantise(o_sb[:], 3, NT, oq, "oq")
            dve.wait_ge(s["wo_sc"], 1)
            dve.wait_ge(s["x_bo"], 1)
            ready = []
            for t in range(NT):
                dve.wait_ge(s["o_mm"], t + 1)
                v.scalar_tensor_tensor(proj[:, t, :], bank(2 + t % 2, C), scale[:, 3, t:t + 1], wo_scale[:],
                                       ALU.mult, ALU.mult).then_inc(s["o_read"], 1)
                dve.wait_ge(s["o_read"], t + 1)
                ready.append(mark(v.tensor_tensor(x2[:, t, :], proj[:, t, :], x_bo[:, t, :], ALU.add)))
            layer_norm(x2, 1)

            r = lambda ap: ap.unsqueeze(2)
            dve.wait_ge(s["lg_mm"], NT)
            lg = bank(6, NT * E).rearrange("p (t e) -> p t e", t=NT)
            after(mark(v.tensor_reduce(r_max[:], lg, AX.X, ALU.max)))
            v.tensor_tensor(r_e[:], lg, r(r_max[:]).to_broadcast([P, NT, E]), ALU.subtract).then_inc(s["lg_sub"], 1)
            dve.wait_ge(s["lg_exp"], 1)
            after(mark(v.tensor_reduce(r_sum[:, 0, :], r_e[:], AX.X, ALU.add)))
            after(mark(v.reciprocal(r_sum[:, 0, :], r_sum[:, 0, :])))
            dve.wait_ge(s["const_pad"], 2)
            after(mark(v.tensor_tensor(r_p[:, :, 0:E], r_e[:], r(r_sum[:, 0, :]).to_broadcast([P, NT, E]), ALU.mult)))
            for t in range(NT):
                c = mark(v.max(r_top[:, t, :], r_p[:, t, 0:E]))
            after(c)

            def inverse_sum(src, row):
                total = r_sum[:, row, :]
                after(mark(v.tensor_reduce(total, src, AX.X, ALU.add)))
                after(mark(v.tensor_scalar(total, total, 1e-12, None, ALU.max)))
                after(mark(v.reciprocal(total, total)))

            inverse_sum(r_top[:], 1)
            after(mark(v.tensor_tensor(r_ren[:], r_top[:], r(r_sum[:, 1, :]).to_broadcast([P, NT, TOPK]), ALU.mult)))
            for t in range(NT):
                c = mark(v.tensor_tensor_scan(r_cum[:, t, :], r_ren[:, t, :], r_zero[:], 0.0, ALU.add, ALU.add))
            after(c)
            after(mark(v.tensor_scalar(r_act[:, :, 1:TOPK], r_cum[:, :, 0:TOPK - 1], KEEP, None, ALU.is_lt)))
            after(mark(v.tensor_tensor(r_rw[:], r_top[:], r_act[:], ALU.mult)))
            after(mark(v.scalar_tensor_tensor(r_find[:], r_act[:], -1.0, r_rw[:], ALU.add, ALU.add)))
            for t in range(NT):
                mark(v.match_replace(r_rep[:, t, :], r_find[:, t, :], r_p[:, t, :], -2.0))
            inverse_sum(r_rw[:], 2)
            after(mark(v.scalar_tensor_tensor(comb[:], r_rep[:, :, 0:E], -1.5, r_p[:, :, 0:E], ALU.is_lt, ALU.mult)))
            for t in range(NT):
                v.tensor_scalar(comb3[:, t, :, :], comb[:, t, :].unsqueeze(1).to_broadcast([P, 3, E]),
                                r_sum[:, 2, t:t + 1], None, ALU.mult).then_inc(s["comb"], 1)
            dve.wait_ge(s["comb_sb"], 1)
            ct, cp = comb_t[0:3 * E, :], comb_part[0:3 * E, :]
            for a in range(2):
                after(mark(v.tensor_copy(cp, ct)))
                after(mark(v.scalar_tensor_tensor(ct, cp, part_step[0:3 * E, a:a + 1], ct, ALU.mult, ALU.add)))
            v.tensor_copy(cp, ct).then_inc(s["comb_part"], 1)

            def gate_up(j, sl):
                dve.wait_ge(s["u_mm"], j + 1)
                dve.wait_ge(s["silu"], j + 1)
                v.tensor_tensor(gated[:, sl, :], silu[:, sl, :], bank(2 + sl), ALU.mult).then_inc(s["gated"], 1)

            def weigh(j, sl):
                dve.wait_ge(s["gated"], j + 1)
                dve.wait_ge(s["ce_mm"], j + 1)
                wait(dve, "hid_hi", j - 1)
                v.tensor_tensor(hid[:, sl, :], gated[:, sl, :], bank(4 + sl), ALU.mult).then_inc(s["hid"], 1)

            def hidden_lo(j, sl):
                dve.wait_ge(s["hid_hi"], j + 1)
                wait(dve, "dn_mm", j - 1)
                v.tensor_tensor(hid_lo[:, sl, :], hid[:, sl, :], fr(hid_hi[:, sl, :]), ALU.subtract).then_inc(s["hid_lo"], 1)

            gate_up(0, 0)
            gate_up(1, 1)
            weigh(0, 0)
            hidden_lo(0, 0)
            with dve.Fori(1, FT // 2) as i:
                for sl in range(2):
                    gate_up(i * 2 + sl, sl)
                    weigh(i * 2 + (sl - 1), 1 - sl)
                    hidden_lo(i * 2 + (sl - 1), 1 - sl)
            weigh(FT - 1, 1)
            hidden_lo(FT - 1, 1)
            for t in range(NT):
                dve.wait_ge(s["y_mm"], t // 2 * 2 + 2)
                v.tensor_tensor(y_sb[:, t, :], ps[:, 6 + t // 2, (t % 2) * C:(t % 2 + 1) * C], x2[:, t, :],
                                ALU.add).then_inc(s["y_done"], 1)

        @block.tensor
        def _(pe):
            mm = nc.tensor.matmul

            def product(acc, terms):
                for i, (lhs, rhs) in enumerate(terms):
                    ins = mm(acc, lhs, rhs, start=(i == 0), stop=(i == len(terms) - 1))
                return ins

            def key_proj(i):
                gi, b = i // B, i % B
                wait(pe, "k_act", i - 1)
                pe.wait_ge(s["ctx_lo"], CK * (b + 1))
                at = slice(b * L, (b + 1) * L)
                product(bank(i % 2), [
                    (w[:, k * G + gi].rearrange("p a c -> p (a c)"), c[:, k, at])
                    for k in range(CK) for w, c in ((wk_hi, ctx_hi), (wk_hi, ctx_lo), (wk_lo, ctx_hi))
                ]).then_inc(s["k_mm"], 1)

            def transposes(dst, src, tiles):
                for t in range(tiles):
                    for k in range(CK):
                        ins = nc.tensor.transpose(dst[:, k, t * P:(t + 1) * P], src[:, t, k * P:(k + 1) * P], ident_bf[:])
                return ins

            pe.wait_ge(s["wk_lo"], 1)
            for i in range(5):
                key_proj(i)
            pe.wait_ge(s["const_ident"], 3)
            pe.wait_ge(s["xq"], NT)
            transposes(bank_bf(4, CK * TOK).rearrange("p (k n) -> p k n", k=CK), xq, NT).then_inc(s["xq_tp"], 1)
            pe.wait_ge(s["wqq"], CK)
            transposes(bank_bf(5, CK * C).rearrange("p (k n) -> p k n", k=CK), wqq, CK).then_inc(s["w_tp"], 1)
            pe.wait_ge(s["woq"], CK)
            for t in range(NT):
                nc.tensor.transpose(ps[0:1, 6, t * P:(t + 1) * P], scale[:, 0, t:t + 1], ident[:])
            for w in range(2):
                for k in range(CK):
                    ins = nc.tensor.transpose(ps[0:1, 7, w * C + k * P:w * C + (k + 1) * P], scale[:, 1 + w, k:k + 1], ident[:])
            ins.then_inc(s["row_tp"], 1)
            for i in range(5, G * B):
                key_proj(i)
            pe.wait_ge(s["xq_t"], 1)
            transposes(bank_bf(4, CK * C).rearrange("p (k n) -> p k n", k=CK), woq, CK).then_inc(s["w_tp"], 1)
            pe.wait_ge(s["rows"], 1)
            pe.wait_ge(s["wqq_t"], 1)
            for i in range(G):
                wait(pe, "qs_sb", i - 1)
                mm(bank(6 + i % 2), wq_scale_row[:, i].rearrange("p a c -> p (a c)"), x_scale_row[:], start=True, stop=True).then_inc(s["outer_mm"], 1)
                if i < 2:
                    pe.wait_ge(s["k_act"], G * B - 1 + i)
                wait(pe, "q_acc_read", i - 1)
                product(bank(i % 2), [(wqq_t[:, k * G + i].rearrange("p a c -> p (a c)"), xq_t[:, k, :]) for k in range(CK)]).then_inc(s["q_mm"], 1)
            mm(bank(5, C), ones_row[:], wo_scale_row[:], start=True, stop=True).then_inc(s["wo_sc_mm"], 1)
            pe.wait_ge(s["wv_lo"], 1)
            for i in range(B * LC):
                wait(pe, "v_done", i - 1)
                at = slice(i * P, (i + 1) * P)
                product(bank(2 + i % 2, C), [
                    (c[:, k, at], w[:, k, :])
                    for k in range(CK) for w, c in ((wv_hi, ctx_hi), (wv_lo, ctx_hi), (wv_hi, ctx_lo))
                ]).then_inc(s["v_mm"], 1)

            def scores(h, t):
                n = h * NT + t
                pe.wait_ge(s["qm"], h * (NT // 2) + (t // 2 + 1))
                wait(pe, "sm", n - 1)
                kb = key[:, group_at(h, B * L, t // NTB * L, L)]
                at = slice(t * P, (t + 1) * P)
                product(bank(t % 2), [(qm_hi[:, at], kb), (qm_lo[:, at], kb)]).then_inc(s["score"], 1)

            def transpose_probs(h, t):
                n = h * NT + t
                pe.wait_ge(s["expd"], n + 1)
                wait(pe, "pt_lo", n - 3)
                for k in range(LC):
                    at = slice(k * P, (k + 1) * P)
                    ins = nc.tensor.transpose(ps[:, PT_BANKS[t], at], prob[:, t, at], ident[:])
                ins.then_inc(s["pt_mm"], 1)

            def values(h, hh, b):
                pe.wait_ge(s["pt_lo"], h * NT + (b * NTB + NTB))
                pe.wait_ge(s["v_split"], h + 1)
                for k in range(LC):
                    for pt in (pt_hi, pt_lo):
                        ins = mm(ps[:, 5, b * N:(b + 1) * N], val_head[:, hh, b * LC + k], pt[:, b, k, :],
                                 start=(hh == 0 and b == 0 and k == 0 and pt is pt_hi),
                                 stop=(hh == HG - 1 and k == LC - 1 and pt is pt_lo), skip_group_check=True)
                ins.then_inc(s["pv"], 1)

            def transpose_out(gr):
                pe.wait_ge(s["ot"], gr + 1)
                pe.wait_ge(s["out_got"], gr + 1)
                for t in range(NT):
                    ins = mm(ps[:, 7, t * GC:(t + 1) * GC], ot_sb[:, t * P:(t + 1) * P], hi_lo_sum[:], start=True, stop=True)
                ins.then_inc(s["out_tp"], 1)

            def group(gr, first=False):
                for hh in range(HG):
                    h = gr * HG + hh
                    start = first and hh == 0
                    for t in range(NT):
                        scores(h, t)
                        if t >= 2:
                            transpose_probs(h, t - 2)
                        elif not start:
                            transpose_probs(h - 1, t + 2)
                        if t == 0 and not (first and hh < 2):
                            values(h - 2, (hh - 2) % HG, 1)
                        if t == 2 and not start:
                            if hh == 1 and not first:
                                pe.wait_ge(s["ot"], gr)
                            values(h - 1, (hh - 1) % HG, 0)
                        if hh == 1 and t == 3 and not first:
                            transpose_out(gr - 1)

            pe.wait_ge(s["q_acc_read"], G)
            pe.wait_ge(s["k_done"], G * B)
            pe.wait_ge(s["v_done"], B * LC)
            pe.wait_ge(s["qs_sb"], G)
            pe.wait_ge(s["woq_t"], 1)
            pe.wait_ge(s["wo_sc"], 1)
            group(0, True)
            with pe.Fori(1, G) as gr:
                group(gr)
            transpose_probs(H - 1, 2)
            values(H - 2, HG - 2, 1)
            transpose_probs(H - 1, 3)
            values(H - 1, HG - 1, 0)
            values(H - 1, HG - 1, 1)
            transpose_out(G - 1)

            def out_proj(t):
                pe.wait_ge(s["oq_t"], t + 1)
                wait(pe, "o_read", t - 1)
                product(bank(2 + t % 2, C), [(oq_t[:, t, k, :], woq_t[:, k, :]) for k in range(CK)]).then_inc(s["o_mm"], 1)

            def logits(t):
                pe.wait_ge(s["xn_hi"], t + 1)
                for k in range(CK):
                    ins = mm(ps[:, 6, t * E:(t + 1) * E], xn_t[:, k, t * P:(t + 1) * P], gate_sb[:, k, :],
                             start=(k == 0), stop=(k == CK - 1))
                ins.then_inc(s["lg_mm"], 1)

            for t in range(NT):
                pe.wait_ge(s["oq"], t + 1)
                wait(pe, "oq_t", t - 1)
                tp = bank_bf(t % 2, CK * P).rearrange("p (k n) -> p k n", k=CK)
                for k in range(CK):
                    ins = nc.tensor.transpose(tp[:, k, :], oq[:, t, k * P:(k + 1) * P], ident_bf[:])
                ins.then_inc(s["oq_tp"], 1)
                if t:
                    out_proj(t - 1)
            out_proj(NT - 1)

            pe.wait_ge(ld["gate"], 16)
            for t in range(NT):
                pe.wait_ge(s["xn2"], t + 1)
                wait(pe, "xn_hi", t - 1)
                for k in range(CK):
                    ins = nc.tensor.transpose(ps[:, 4 + t % 2, k * P:(k + 1) * P], xn[:, t, k * P:(k + 1) * P], ident[:])
                ins.then_inc(s["xn_tp"], 1)
                if t:
                    logits(t - 1)
            logits(NT - 1)

            def gate_and_up(j, sl):
                pe.wait_ge(s["gu_split"], j + 1)
                for u, freed, done in ((0, "silu", "g_mm"), (1, "gated", "u_mm")):
                    wait(pe, freed, j - 1)
                    product(bank(2 * u + sl), [
                        (w[:, sl, (2 * k + u) * P:(2 * k + u + 1) * P], xt[:, k, :])
                        for k in range(CK) for w, xt in ((w_hi_gu, xn_hi), (w_lo_gu, xn_hi), (w_hi_gu, xn_lo))
                    ]).then_inc(s[done], 1)

            def token_weights(j, sl):
                wait(pe, "hid", j - 1)
                mm(bank(4 + sl), expert_sel[0:3 * E, bass.ds(j * P, P)], comb_part[0:3 * E, :], start=True, stop=True).then_inc(s["ce_mm"], 1)

            def down(j, sl, first=False, last=False):
                pe.wait_ge(s["hid_lo"], j + 1)
                pe.wait_ge(s["dn_split"], j + 1)
                for t in range(NT):
                    at = slice(t * P, (t + 1) * P)
                    acc = ps[:, 6 + t // 2, (t % 2) * C:(t % 2 + 1) * C]
                    terms = ((hid_hi, w_hi_dn), (hid_hi, w_lo_dn), (hid_lo, w_hi_dn))
                    for i, (hd, w) in enumerate(terms):
                        ins = mm(acc, hd[:, sl, at], w[:, sl, :], start=(first and i == 0 and t % 2 == 0),
                                 stop=(last and i == 2), skip_group_check=True)
                    if last:
                        ins.then_inc(s["y_mm"], 1)
                if not last:
                    ins.then_inc(s["dn_mm"], 1)

            pe.wait_ge(s["xn_lo"], NT)
            gate_and_up(0, 0)
            for t in range(NT):
                pe.wait_ge(s["comb"], t + 1)
                ins = nc.tensor.transpose(ps[0:3 * E, 7, t * P:(t + 1) * P], comb3[:, t].rearrange("p a e -> p (a e)"), ident[:])
            ins.then_inc(s["comb_tp"], 1)
            gate_and_up(1, 1)
            pe.wait_ge(s["comb_part"], 1)
            pe.wait_ge(s["sel"], 1)
            token_weights(0, 0)
            gate_and_up(2, 0)
            token_weights(1, 1)
            down(0, 0, first=True)
            gate_and_up(3, 1)
            token_weights(2, 0)
            down(1, 1)
            with pe.Fori(2, FT // 2) as i:
                for sl in range(2):
                    gate_and_up(i * 2 + sl, sl)
                    token_weights(i * 2 + (sl - 1), 1 - sl)
                    down(i * 2 + (sl - 2), sl)
            token_weights(FT - 1, 1)
            down(FT - 2, 0)
            down(FT - 1, 1, last=True)


def kernel(**inputs):
    import numpy as np
    import concourse.bacc as bacc
    from concourse.bass_utils import run_bass_kernel_spmd

    a = {k: np.asarray(v) for k, v in inputs.items()}
    gu = a["L0_ffn_gate_up_proj"].reshape(E, 2, INTER, CK, P)
    gu = gu.transpose(4, 3, 1, 0, 2).reshape(P, CK, 2, FT, P)
    arrays = {
        "x": a["x"].reshape(TOK, C),
        "ctx_t": a["ctx_2048"].reshape(B * L, C).T,
        "mask": a["mask_BxSxS2_ff0"],
        "wq": a["L0_xattn_wq"],
        "bq_t": a["L0_xattn_bq"].reshape(G, GC).T,
        "wk_t": a["L0_xattn_wk"].T,
        "bk_t": a["L0_xattn_bk"].reshape(G, GC).T,
        "wv_t": a["L0_xattn_wv"].T,
        "bv": a["L0_xattn_bv"],
        "wo": a["L0_xattn_wo"],
        "bo": a["L0_xattn_bo"],
        "gate_t": a["L0_ffn_gate_weight"].T,
        "gu_t": gu.transpose(0, 3, 1, 2, 4).reshape(P, FT, WGU),
        "down_t": a["L0_ffn_down_proj"].transpose(0, 2, 1).reshape(FT, P, C).transpose(1, 0, 2),
    }
    nc = bacc.Bacc("TRN2", target_bir_lowering=False, num_devices=1)
    arrays = {f"in_{k}": np.ascontiguousarray(v) for k, v in arrays.items()}
    args = [nc.dram_tensor(k, v.shape, mybir.dt.from_np(v.dtype), kind="ExternalInput").ap() for k, v in arrays.items()]
    out = nc.dram_tensor("out_0", (B, N, C), F32, kind="ExternalOutput").ap()
    build(nc, *args, out)
    return run_bass_kernel_spmd(nc, [arrays], core_ids=[0]).results[0]["out_0"]
```

```python
from contextlib import ExitStack

import concourse.bass as bass
from concourse import mybir

F32 = mybir.dt.float32
F32R = mybir.dt.float32r
BF16 = mybir.dt.bfloat16
ALU = mybir.AluOpType
ACT = mybir.ActivationFunctionType
AX = mybir.AxisListType

P = 128
B, N, L, C = 2, 256, 512, 256
H = 16
D = C // H
TOK = B * N
NT = TOK // P
NTB = N // P
CK = C // P
LC = L // P
HG = 4
G = H // HG
GC = HG * D
E, INTER, TOPK = 32, 96, 8
FT = E * INTER // P
WGU = CK * 2 * P
WRAW = WGU + C
V_BANKS = (7, 4)
V_EARLY = 4
PT_BANKS = (2, 3, 4, 6)
XT_BANKS = (4, 5, 2, 3)
FILLERS = 8
KEEP = 0.8
LN_EPS = 1e-5
Q_EPS = 1e-8
QMAX = 127.0
ROUND = 12582912.0
BIG = 3.0e38


def build(nc, x, ctx_t, mask, wq, bq_t, wk_t, bk_t, wv_t, bv, wo, bo, gate_t, gu_t, down_t, out):
    with ExitStack() as stack:
        def sem(name):
            return stack.enter_context(nc.semaphore(name))

        def sb_in(scope, name, shape, dt=F32):
            return scope.enter_context(nc.sbuf_tensor(name, shape, dt))

        def sb(name, shape, dt=F32):
            return sb_in(stack, name, shape, dt)

        ident = sb("ident", [P, P])
        ident_bf = sb("ident_bf", [P, P], BF16)
        ones_row = sb("ones_row", [1, P])
        act_warm = sb("act_warm", [1, 4])
        hi_lo_sum = sb("hi_lo_sum", [P, GC])
        head_band = sb("head_band", [P, 2, H])
        head_mask = sb("head_mask", [P, H])
        part_col = sb("part_col", [P, 1])
        part_step = sb("part_step", [P, 1])
        expert_of = sb("expert_of", [P, FT * P], BF16)
        part_mod = sb("part_mod", [P, 1])
        expert_sel = sb("expert_sel", [P, FT * P], BF16)
        x_sb = sb("x_sb", [P, NT, C])
        x_bo = x_sb
        x2 = x_sb
        xn = sb("xn", [P, NT, C])
        wo_sb = sb("wo_sb", [P, CK, C])
        woq = sb("woq", [P, CK, C], BF16)
        woq_t = sb("woq_t", [P, CK, C], BF16)
        wq_scale_col = sb("wq_scale_col", [P, G])
        wo_scale_row = sb("wo_scale_row", [1, C])
        wo_scale = sb("wo_scale", [P, C])
        gate_sb = sb("gate_sb", [P, CK, E])
        bq_sb = sb("bq_sb", [P, G])
        bk_sb = sb("bk_sb", [P, CK])
        bo_sb = sb("bo_sb", [P, C])
        ln_stats = sb("ln_stats", [P, 2, NT, 6])
        ln_mv = sb("ln_mv", [P, 2, NT, 2])
        ln_var = sb("ln_var", [P, 2, NT])
        ln_std = sb("ln_std", [P, 2, NT])
        ln_rstd = sb("ln_rstd", [P, 2, NT])
        amax = sb("amax", [P, 4, NT])
        scale = sb("scale", [P, 4, NT])
        rscale = sb("rscale", [P, 4, NT])
        o_max = sb("o_max", [P, 2, NT])
        neg_max = sb("neg_max", [P, NT])
        p_sum = sb("p_sum", [P, NT, H])
        o_sb = sb("o_sb", [P, NT, C])
        ot_sb = sb("ot_sb", [P, TOK])
        r_max = sb("r_max", [P, NT])
        r_sum = sb("r_sum", [P, 3, NT])
        r_p = sb("r_p", [P, NT, E + TOPK])
        r_act = sb("r_act", [P, NT, TOPK])
        r_zero = sb("r_zero", [P, TOPK])

        first = ExitStack()

        def sb(name, shape, dt=F32):
            return sb_in(first, name, shape, dt)

        ctx_sb = sb("ctx_sb", [P, CK, B * L])
        ctx_hi = sb("ctx_hi", [P, CK, B * L], F32R)
        ctx_lo = sb("ctx_lo", [P, CK, B * L], F32R)
        wv_sb = sb("wv_sb", [P, CK, C])
        wv_hi = sb("wv_hi", [P, CK, C], F32R)
        wv_lo = sb("wv_lo", [P, CK, C], F32R)
        bv_sb = sb("bv_sb", [P, C])
        wk_sb = sb("wk_sb", [P, CK, C])
        wk_hi = sb("wk_hi", [P, CK, C], F32R)
        wk_lo = sb("wk_lo", [P, CK, C], F32R)
        wq_sb = sb("wq_sb", [P, CK, C])
        wqq = sb("wqq", [P, CK, C], BF16)
        wqq_t = sb("wqq_t", [P, CK * G, 2, GC], BF16)
        xq = sb("xq", [P, NT, C], BF16)
        xq_t = sb("xq_t", [P, CK, TOK], BF16)
        x_scale_row = sb("x_scale_row", [1, TOK])
        wq_scale_row = sb("wq_scale_row", [1, G, 2, GC])
        first.close()

        w_raw_gu = sb_in(stack, "w_raw_gu", [P, FT, WGU])

        second = ExitStack()

        def sb(name, shape, dt=F32):
            return sb_in(second, name, shape, dt)

        prob = sb("prob", [P, NT, L])
        pt_hi = sb("pt_hi", [P, B, LC, N], F32R)
        pt_lo = sb("pt_lo", [P, B, LC, N], F32R)
        mask_sb = sb("mask_sb", [P, NT, L])
        key = sb("key", [P, G * B * L], F32R)
        val = sb("val", [P, B * LC, H, D])
        val_head = sb("val_head", [P, HG, B * LC, HG * 2 * D], F32R)
        q_hi = sb("q_hi", [P, G * TOK], F32R)
        q_lo = sb("q_lo", [P, G * TOK], F32R)
        qm_hi = sb("qm_hi", [P, TOK], F32R)
        qm_lo = sb("qm_lo", [P, TOK], F32R)
        neg_s = sb("neg_s", [P, NT, L])
        second.close()
        q_f, x_scale_all = neg_s, ot_sb

        def sb(name, shape, dt=F32):
            return sb_in(stack, name, shape, dt)

        w_raw_dn = sb("w_raw_dn", [P, FT, C])
        oq = sb("oq", [P, NT, C], BF16)
        oq_t = sb("oq_t", [P, NT, CK, P], BF16)
        proj = sb("proj", [P, NT, C])
        xn_t = sb("xn_t", [P, CK, TOK])
        xn_hi = sb("xn_hi", [P, CK, TOK], F32R)
        xn_lo = sb("xn_lo", [P, CK, TOK], F32R)
        r_e = sb("r_e", [P, NT, E])
        r_top = sb("r_top", [P, NT, TOPK])
        r_ren = sb("r_ren", [P, NT, TOPK])
        r_cum = sb("r_cum", [P, NT, TOPK])
        r_rw = sb("r_rw", [P, NT, TOPK])
        r_find = sb("r_find", [P, NT, TOPK])
        r_rep = sb("r_rep", [P, NT, E + TOPK])
        p_part = sb("p_part", [P, 2, NT, E], BF16)
        p_rest = sb("p_rest", [P, 2, NT, E])
        comb3 = sb("comb3", [P, NT, 3, E], BF16)
        comb_part = sb("comb_part", [P, TOK], BF16)
        w_hi_gu = sb("w_hi_gu", [P, 2, WGU], F32R)
        w_lo_gu = sb("w_lo_gu", [P, 2, WGU], F32R)
        w_hi_dn = sb("w_hi_dn", [P, 2, C], F32R)
        w_lo_dn = sb("w_lo_dn", [P, 2, C], F32R)
        silu = sb("silu", [P, 2, TOK])
        gated = sb("gated", [P, 2, TOK])
        hid = sb("hid", [P, 2, TOK])
        hid_hi = sb("hid_hi", [P, 2, TOK], F32R)
        hid_lo = sb("hid_lo", [P, 2, TOK], F32R)
        y_sb = sb("y_sb", [P, NT, C])

        ps = stack.enter_context(nc.psum_tensor("ps", [P, 8, 512], F32))

        def bank(i, n=512, rows=P):
            return ps[0:rows, i, 0:n]

        def bank_bf(i, n):
            return ps[:, i, 0:n // 2].bitcast(BF16)

        loads = ["x", "ctx0", "ctx1", "mask", "wq", "wo", "wk", "wv", "bq", "bk", "bv", "bo", "gate"]
        ld = {n: sem("ld_" + n) for n in loads}
        NGU = 4
        ld_gu = [sem(f"ld_gu{i}") for i in range(NGU)]
        ld_dn = sem("ld_dn")
        names = """ce_mm comb comb_part comb_tp const_ident const_mask const_pad const_sel const_zero
            ctx_hi ctx_lo dn_hi dn_mm dn_split dve_step expd g_mm gated gu_hi gu_split hid hid_hi
            hid_lo k_hi k_lo k_mm lg_exp lg_mm lg_sub o_mm o_read oq oq_t oq_tp ot out_got out_tp p_inv p_rest
            pool_step pool_turn pt_hi pt_lo pt_mm pv q_f q_hi q_lo q_mm q_scales q_scales_mm qm r_p rows score
            sel silu sm sm_turn std stored u_mm v_hi v_done v_mm v_sb v_split var w_tp wk_hi wk_lo wo_row
            wo_row_tp wo_sc wo_sc_mm wo_tp woq woq_t wqq wqq_t wv_hi wv_lo x2 x_bo x_row x_row_tp x_scale_mm xn1 xn2 xn_hi xn_lo
            xn_t xn_tp xq xq_t xq_tp y_done y_mm""".split()
        s = {n: sem("s_" + n) for n in names}

        block = stack.enter_context(nc.Block())

        def twice(ap):
            ap = ap.rearrange("p (g c) -> p g c", c=GC)
            return ap.unsqueeze(2).to_broadcast([ap.shape[0], ap.shape[1], 2, GC])

        def group_at(h, width, start, n):
            return bass.ds((h & (H - HG)) * (width // HG) + start, n)

        def at_head(h):
            return bass.ds(h, 1)

        def key_half(i):
            bk, half = i // 2, i % 2
            b, pair = bk // CK, bk % CK
            rows = slice(half * GC, (half + 1) * GC)
            other = slice((1 - half) * GC, (2 - half) * GC)
            at = ((pair * 2 + half) * B + b) * L
            return ps[rows, bk, :], rows, other, slice(at, at + L), bk_sb[rows, pair:pair + 1]

        def pt_bank(t):
            return bank(PT_BANKS[t]).rearrange("p (k n) -> p k n", k=LC)

        def xt_bank(t):
            return bank(XT_BANKS[t], CK * P).rearrange("p (k n) -> p k n", k=CK)

        def pt_cols(buf, t):
            return buf[:, t // NTB, :, (t % NTB) * P:(t % NTB + 1) * P]

        def fr(ap):
            return ap.bitcast(F32)

        def wait(eng, name, count):
            if not isinstance(count, int) or count > 0:
                eng.wait_ge(s[name], count)

        x_dram = x.rearrange("(t p) c -> p t c", p=P)
        ctx_dram = ctx_t.rearrange("(k p) n -> p k n", p=P)
        out_dram = out.rearrange("b (t p) c -> p (b t) c", p=P)

        @block.sync
        def _(sp):
            sp.dma_start(x_sb[:], x_dram).then_inc(ld["x"], 16)
            sp.dma_start(ctx_sb[:, :, 0:L], ctx_dram[:, :, 0:L]).then_inc(ld["ctx0"], 16)
            sp.dma_start(ctx_sb[:, :, L:2 * L], ctx_dram[:, :, L:2 * L]).then_inc(ld["ctx1"], 16)
            sp.dma_start(bk_sb[:], bk_t).then_inc(ld["bk"], 16)
            for half in range(2):
                sp.dma_start(bq_sb[half * GC:(half + 1) * GC, :], bq_t).then_inc(ld["bq"], 16)
            sp.dma_start(bv_sb[:], bv.partition_broadcast(P)).then_inc(ld["bv"], 16)
            sp.dma_start(mask_sb[:], mask.rearrange("b (t p) l -> p (b t) l", p=P)).then_inc(ld["mask"], 16)
            sp.dma_start(wo_sb[:], wo.rearrange("(k p) n -> p k n", p=P)).then_inc(ld["wo"], 16)
            sp.dma_start(bo_sb[:], bo.partition_broadcast(P)).then_inc(ld["bo"], 16)
            sp.dma_start(gate_sb[:], gate_t.rearrange("(k p) n -> p k n", p=P)).then_inc(ld["gate"], 16)
            sp.wait_ge(s["v_done"], B * LC)
            sp.wait_ge(s["k_lo"], G * B)
            sp.wait_ge(s["q_lo"], G)
            for i in range(NGU):
                cut = slice(i * FT // NGU, (i + 1) * FT // NGU)
                sp.dma_start(w_raw_gu[:, cut, :], gu_t[:, cut, :]).then_inc(ld_gu[i], 16)
            sp.wait_ge(s["pv"], H * B)
            sp.dma_start(w_raw_dn[:], down_t).then_inc(ld_dn, 16)
            for t in range(NT):
                sp.wait_ge(s["y_done"], t + 1)
                sp.dma_start(out_dram[:, t, :], y_sb[:, t, :]).then_inc(s["stored"], 16)
            sp.wait_ge(s["stored"], 16 * NT)

        @block.gpsimd
        def _(pool):
            g = nc.gpsimd
            n = [0]

            def step(ins):
                n[0] += 1
                ins.then_inc(s["pool_step"], 1)
                pool.wait_ge(s["pool_step"], n[0])

            step(g.memset(ident[:], 0.0))
            g.affine_select(out=ident[:], in_=ident[:], compare_op=ALU.not_equal, fill=1.0, base=0,
                            pattern=[[-1, P]], channel_multiplier=1).then_inc(s["const_ident"], 1)
            pool.wait_ge(s["const_ident"], 1)
            g.tensor_copy(ident_bf[:], ident[:]).then_inc(s["const_ident"], 1)
            g.memset(ones_row[:], 1.0).then_inc(s["const_ident"], 1)

            step(g.memset(head_band[:], 1.0))
            band = head_band[:].rearrange("p d (a h) -> p d a h", h=HG)
            step(g.affine_select(out=band, in_=band, compare_op=ALU.is_ge, fill=0.0, base=0,
                                 pattern=[[-GC, 2], [0, G], [-D, HG]], channel_multiplier=1))
            step(g.affine_select(out=band, in_=band, compare_op=ALU.is_ge, fill=0.0, base=D - 1,
                                 pattern=[[GC, 2], [0, G], [D, HG]], channel_multiplier=-1))
            g.tensor_tensor(head_mask[:], head_band[:, 0, :], head_band[:, 1, :], ALU.add).then_inc(s["const_mask"], 1)
            eye = ident[:].rearrange("p (h a d) -> p h a d", h=HG, a=2)
            g.tensor_tensor(hi_lo_sum[:].rearrange("p (h d) -> p h d", h=HG), eye[:, :, 0, :], eye[:, :, 1, :],
                            ALU.add).then_inc(s["const_mask"], 1)

            def low(lo, full, hi, done):
                g.tensor_tensor(lo, full, fr(hi), ALU.subtract).then_inc(s[done], 1)

            pool.wait_ge(s["wk_hi"], 1)
            low(wk_lo[:], wk_sb[:], wk_hi[:], "wk_lo")
            for b in range(B):
                for k in range(CK):
                    pool.wait_ge(s["ctx_hi"], b + 1)
                    at = slice(b * L, (b + 1) * L)
                    low(ctx_lo[:, k, at], ctx_sb[:, k, at], ctx_hi[:, k, at], "ctx_lo")
            pool.wait_ge(s["wv_hi"], 1)
            low(wv_lo[:], wv_sb[:], wv_hi[:], "wv_lo")
            g.memset(fr(val_head[:]), 0.0).then_inc(s["const_zero"], 1)
            g.memset(r_zero[:], 0.0)
            g.memset(r_act[:], 1.0)
            g.memset(r_p[:], -1.0).then_inc(s["const_pad"], 1)

            def value_out(i):
                pool.wait_ge(s["v_sb"], i + 1)
                g.tensor_tensor(val[:, i], val[:, i],
                                bv_sb[:].rearrange("p (h d) -> p h d", h=H), ALU.add).then_inc(s["v_done"], 1)

            pool.wait_ge(s["const_mask"], 1)

            def mask_query(h, m):
                wait(pool, "score", h * NT + (2 * m + 2 - NT))
                pool.sem_inc(s["pool_turn"], 1)
                cols = slice(m * 2 * P, (m + 1) * 2 * P)
                hm = head_mask[:, bass.ds(h, 1)].to_broadcast([P, 2 * P])
                for qm, q in ((qm_hi, q_hi), (qm_lo, q_lo)):
                    ins = g.tensor_tensor(qm[:, cols], fr(q[:, group_at(h, TOK, m * 2 * P, 2 * P)]), hm, ALU.mult)
                ins.then_inc(s["qm"], 1)

            pool.wait_ge(s["q_lo"], 1)
            for m in range(NT // 2):
                mask_query(0, m)
            pool.wait_ge(ld["bv"], 16)
            for i in range(V_EARLY):
                value_out(i)

            def split_values(h, hh):
                wait(pool, "pv", h * B + (B - HG * B))
                wait(pool, "v_hi", h + (1 - HG))
                pool.sem_inc(s["pool_turn"], 1)
                v = val[:, :, bass.ds(h, 1), :].squeeze(2)
                lo = (hh * 2 + 1) * D
                hi_cols = val_head[:, hh, :, lo - D:lo]
                g.tensor_copy(hi_cols, v).then_inc(s["v_hi"], 1)
                pool.wait_ge(s["v_hi"], h + 1)
                pool.sem_inc(s["pool_turn"], 1)
                g.tensor_tensor(val_head[:, hh, :, lo:lo + D], v, fr(hi_cols), ALU.subtract).then_inc(s["v_split"], 1)

            mask_query(1, 0)
            for i in range(V_EARLY, B * LC - 2):
                value_out(i)
            mask_query(1, 1)
            value_out(B * LC - 2)
            value_out(B * LC - 1)
            pool.wait_ge(s["v_done"], B * LC)
            pool.wait_ge(s["const_zero"], 1)
            for hh in range(HG):
                if hh >= 2:
                    for m in range(NT // 2):
                        mask_query(hh, m)
                split_values(hh, hh)
            pool.wait_ge(s["q_lo"], G)
            with pool.Fori(1, G) as gr:
                for hh in range(HG):
                    for m in range(NT // 2):
                        mask_query(gr * HG + hh, m)
                    split_values(gr * HG + hh, hh)

            pool.wait_ge(ld["x"], 16)
            pool.wait_ge(ld["bo"], 16)
            g.tensor_tensor(x_bo[:], x_sb[:], bo_sb[:].unsqueeze(1).to_broadcast([P, NT, C]), ALU.add).then_inc(s["x_bo"], 1)

            step(g.iota(expert_of[:], pattern=[[1, E], [0, INTER]], base=0, channel_multiplier=0,
                        allow_small_or_imprecise_dtypes=True))
            step(g.iota(part_col[:], pattern=[[0, 1]], base=0, channel_multiplier=1,
                        allow_small_or_imprecise_dtypes=True))
            step(g.tensor_scalar(part_mod[:], part_col[:], 32.0, -32.0, ALU.is_ge, ALU.mult))
            step(g.tensor_tensor(part_mod[:], part_mod[:], part_col[:], ALU.add))
            step(g.tensor_scalar(part_step[:], part_col[:], 64.0, -32.0, ALU.is_ge, ALU.mult))
            g.tensor_tensor(part_mod[:], part_mod[:], part_step[:], ALU.add).then_inc(s["const_sel"], 1)

            def lo_gu(j, sl):
                pool.wait_ge(s["gu_hi"], j + 1)
                pool.sem_inc(s["pool_turn"], 1)
                low(w_lo_gu[:, sl, :], w_raw_gu[:, bass.ds(j, 1), :].squeeze(1), w_hi_gu[:, sl, :], "gu_split")

            def lo_dn(j, sl):
                pool.wait_ge(s["dn_hi"], j + 1)
                pool.sem_inc(s["pool_turn"], 1)
                low(w_lo_dn[:, sl, :], w_raw_dn[:, bass.ds(j, 1), :].squeeze(1), w_hi_dn[:, sl, :], "dn_split")

            lo_gu(0, 0)
            pool.wait_ge(s["x_bo"], 1)
            for t in range(NT):
                pool.wait_ge(s["o_read"], t + 1)
                g.tensor_tensor(x2[:, t, :], proj[:, t, :], x_bo[:, t, :], ALU.add).then_inc(s["x2"], 1)
            lo_gu(1, 1)
            pool.wait_ge(s["r_p"], 1)
            rest = r_p[:, :, 0:E]
            for part in range(2):
                step(g.tensor_copy(p_part[:, part], rest))
                g.tensor_tensor(p_rest[:, part], rest, p_part[:, part], ALU.subtract).then_inc(s["p_rest"], 1)
                pool.wait_ge(s["p_rest"], part + 1)
                rest = p_rest[:, part]
            with pool.Fori(1, FT // 2) as i:
                for sl in range(2):
                    lo_gu(i * 2 + sl, sl)
                    lo_dn(i * 2 + (sl - 2), sl)
            lo_dn(FT - 2, 0)
            lo_dn(FT - 1, 1)

        @block.scalar
        def _(act):
            a = nc.scalar
            dram = lambda w: w.rearrange("(k p) n -> p k n", p=P)
            act.dma_start(wk_sb[:], dram(wk_t)).then_inc(ld["wk"], 16)
            act.dma_start(wq_sb[:], dram(wq)).then_inc(ld["wq"], 16)
            act.dma_start(wv_sb[:], dram(wv_t)).then_inc(ld["wv"], 16)

            act.wait_ge(s["const_ident"], 3)
            a.activation(act_warm[:, 0:1], ones_row[:, 0:1], ACT.Sqrt)
            act.wait_ge(ld["wk"], 16)
            a.copy(wk_hi[:], wk_sb[:]).then_inc(s["wk_hi"], 1)
            act.wait_ge(s["var"], 1)
            a.activation(ln_std[:, 0, :], ln_var[:, 0, :], ACT.Sqrt).then_inc(s["std"], 1)
            act.wait_ge(ld["ctx0"], 16)
            a.copy(ctx_hi[:, :, 0:L], ctx_sb[:, :, 0:L]).then_inc(s["ctx_hi"], 1)
            act.wait_ge(ld["ctx1"], 16)
            a.copy(ctx_hi[:, :, L:2 * L], ctx_sb[:, :, L:2 * L]).then_inc(s["ctx_hi"], 1)
            act.wait_ge(ld["wv"], 16)
            a.copy(wv_hi[:], wv_sb[:]).then_inc(s["wv_hi"], 1)

            act.wait_ge(s["x_row_tp"], 1)
            a.copy(x_scale_row[:], bank(5, TOK, 1)).then_inc(s["x_row"], 1)

            act.wait_ge(ld["bk"], 16)

            def key_hi(i):
                acc, rows, _, cols, bias = key_half(i)
                act.wait_ge(s["k_mm"], i // 2 + 1)
                a.activation(key[rows, cols], acc, ACT.Identity, bias=bias).then_inc(s["k_hi"], 1)

            for i in range(2 * CK * B):
                key_hi(i)
            act.wait_ge(s["w_tp"], 1)
            a.activation(wq_scale_row[:], twice(ps[0:1, 5, C:2 * C]), ACT.Identity, scale=float(D) ** -0.5).then_inc(s["rows"], 1)
            act.wait_ge(s["xq_tp"], 1)
            a.copy(xq_t[:].rearrange("p k n -> p (k n)"), bank_bf(4, CK * TOK)).then_inc(s["xq_t"], 1)
            act.wait_ge(s["x_scale_mm"], 1)
            a.copy(x_scale_all[:], bank(6)).then_inc(s["q_scales"], 1)
            a.activation(act_warm[:, 1:2], ones_row[:, 0:1], ACT.Exp)

            def value_out(i):
                act.wait_ge(s["v_mm"], i + 1)
                a.copy(val[:, i].rearrange("p h d -> p (h d)"), bank(V_BANKS[i % 2], C)).then_inc(s["v_sb"], 1)

            act.wait_ge(s["q_scales_mm"], 1)
            a.copy(wq_scale_col[:], bank(5, G)).then_inc(s["q_scales"], 1)
            value_out(0)
            value_out(1)
            for i in range(G):
                act.wait_ge(s["q_f"], i + 1)
                a.activation(q_hi[:, i * TOK:(i + 1) * TOK], q_f[:, i, :], ACT.Identity,
                             bias=bq_sb[:, i:i + 1]).then_inc(s["q_hi"], 1)
            for i in range(2, V_EARLY):
                value_out(i)

            def exponent(h, t):
                n = h * NT + t
                act.wait_ge(s["sm"], n + 1)
                wait(act, "pt_mm", n - 3)
                a.activation(prob[:, t, :], neg_s[:, t, :], ACT.Exp, bias=neg_max[:, t:t + 1],
                             scale=-1.0, accum_out=p_sum[:, t, at_head(h)]).then_inc(s["expd"], 1)

            def transposed_hi(h, t):
                n = h * NT + t
                act.wait_ge(s["pt_mm"], n + 1)
                wait(act, "pv", h * B + (t // NTB - 1))
                a.copy(pt_cols(pt_hi, t), pt_bank(t)).then_inc(s["pt_hi"], 1)

            def move_out(gr):
                act.wait_ge(s["pv"], gr * (HG * B) + HG * B)
                a.copy(ot_sb[:], bank(5)).then_inc(s["ot"], 1)

            def group(gr, first=False):
                for hh in range(HG):
                    h = gr * HG + hh
                    for t in range(NT):
                        if hh == 1 and t == 2 and not first:
                            move_out(gr - 1)
                        if first and hh == 0 and V_EARLY + t < B * LC:
                            value_out(V_EARLY + t)
                        if t == 3:
                            transposed_hi(h, 0)
                        elif not (first and hh == 0):
                            transposed_hi(h - 1, t + 1)
                        exponent(h, t)

            group(0, True)
            with act.Fori(1, G) as gr:
                group(gr)
            for t in (1, 2, 3):
                transposed_hi(H - 1, t)
            move_out(G - 1)

            def hi_gu(j, sl):
                wait(act, "u_mm", j - 1)
                a.copy(w_hi_gu[:, sl, :], w_raw_gu[:, bass.ds(j, 1), :].squeeze(1)).then_inc(s["gu_hi"], 1)

            def hi_dn(j, sl):
                wait(act, "dn_mm", j - 1)
                a.copy(w_hi_dn[:, sl, :], w_raw_dn[:, bass.ds(j, 1), :].squeeze(1)).then_inc(s["dn_hi"], 1)

            act.wait_ge(s["pv"], H * B)
            act.wait_ge(s["wo_tp"], 1)
            a.copy(woq_t[:].rearrange("p k n -> p (k n)"), bank_bf(2, CK * C)).then_inc(s["woq_t"], 1)
            act.wait_ge(s["wo_row_tp"], 1)
            a.copy(wo_scale_row[:], bank(3, C, 1)).then_inc(s["wo_row"], 1)
            act.wait_ge(ld_gu[0], 16)
            hi_gu(0, 0)
            act.wait_ge(s["wo_sc_mm"], 1)
            a.copy(wo_scale[:], bank(4, C)).then_inc(s["wo_sc"], 1)

            for t in range(NT):
                act.wait_ge(s["oq_tp"], t + 1)
                a.copy(oq_t[:, t].rearrange("p k n -> p (k n)"), bank_bf(t % 2, CK * P)).then_inc(s["oq_t"], 1)
            act.wait_ge(s["var"], 2)
            a.activation(ln_std[:, 1, :], ln_var[:, 1, :], ACT.Sqrt).then_inc(s["std"], 1)
            hi_gu(1, 1)
            for t in range(NT):
                act.wait_ge(s["xn_tp"], t + 1)
                at = slice(t * P, (t + 1) * P)
                a.copy(xn_t[:, :, at], xt_bank(t)).then_inc(s["xn_t"], 1)
                a.copy(xn_hi[:, :, at], xt_bank(t)).then_inc(s["xn_hi"], 1)
            a.activation(act_warm[:, 2:3], ones_row[:, 0:1], ACT.Exp)
            act.wait_ge(s["lg_sub"], 1)
            a.activation(r_e[:], r_e[:], ACT.Exp).then_inc(s["lg_exp"], 1)
            a.activation(act_warm[:, 3:4], ones_row[:, 0:1], ACT.Silu)
            for q in (*ld_gu, ld_dn):
                act.wait_ge(q, 16)
            def silu_of(j, sl):
                act.wait_ge(s["g_mm"], j + 1)
                wait(act, "gated", j - 1)
                a.activation(silu[:, sl, :], bank(sl), ACT.Silu).then_inc(s["silu"], 1)

            def hidden_hi(j, sl):
                act.wait_ge(s["hid"], j + 1)
                wait(act, "dn_mm", j - 1)
                a.copy(hid_hi[:, sl, :], hid[:, sl, :]).then_inc(s["hid_hi"], 1)

            def expert_step(j, sl):
                hi_gu(j + 1, 1 - sl)
                hi_dn(j - 1, 1 - sl)
                silu_of(j, sl)
                hidden_hi(j - 1, 1 - sl)

            hi_dn(0, 0)
            hi_gu(2, 0)
            silu_of(0, 0)
            silu_of(1, 1)
            hi_dn(1, 1)
            hi_gu(3, 1)
            act.wait_ge(s["comb_tp"], 1)
            a.copy(comb_part[0:3 * E, :], bank_bf(7, TOK)[0:3 * E, :]).then_inc(s["comb_part"], 1)
            silu_of(2, 0)
            hi_gu(4, 0)
            hidden_hi(0, 0)
            hidden_hi(1, 1)
            hi_dn(2, 0)
            silu_of(3, 1)
            hidden_hi(2, 0)
            with act.Fori(2, FT // 2 - 1) as i:
                for sl in range(2):
                    expert_step(i * 2 + sl, sl)
            expert_step(FT - 2, 0)
            hi_dn(FT - 2, 0)
            hidden_hi(FT - 2, 0)
            silu_of(FT - 1, 1)
            hi_dn(FT - 1, 1)
            hidden_hi(FT - 1, 1)

        @block.vector
        def _(dve):
            v = nc.vector
            n = [0]

            def mark(ins):
                n[0] += 1
                ins.then_inc(s["dve_step"], 1)
                return n[0]

            def after(count):
                dve.wait_ge(s["dve_step"], count)

            def layer_norm(src, i):
                for t in range(NT):
                    if i:
                        dve.wait_ge(s["x2"], t + 1)
                    c = mark(v.bn_stats(ln_stats[:, i, t, :], src[:, t, :]))
                after(c)
                for t in range(NT):
                    c = mark(v.bn_aggr(ln_mv[:, i, t, :], ln_stats[:, i, t, :]))
                after(c)
                v.tensor_scalar(ln_var[:, i, :], ln_mv[:, i, :, 1], LN_EPS, None, ALU.add).then_inc(s["var"], 1)
                dve.wait_ge(s["std"], i + 1)
                after(mark(v.reciprocal(ln_rstd[:, i, :], ln_std[:, i, :])))
                for t in range(NT):
                    v.tensor_scalar(xn[:, t, :], src[:, t, :], ln_mv[:, i, t, 0:1], ln_rstd[:, i, t:t + 1],
                                    ALU.subtract, ALU.mult).then_inc(s["xn2" if i else "xn1"], 1)

            def quantise(src, i, tiles, dst, done, amax_found=False):
                if not amax_found:
                    after(mark(v.tensor_reduce(amax[:, i, 0:tiles], src, AX.X, ALU.max, apply_absolute_value=True)))
                after(mark(v.tensor_scalar(scale[:, i, 0:tiles], amax[:, i, 0:tiles], 1.0 / QMAX, Q_EPS, ALU.mult, ALU.max)))
                after(mark(v.reciprocal(rscale[:, i, 0:tiles], scale[:, i, 0:tiles])))
                for pair in range(0, tiles, 2):
                    ts = (pair, pair + 1)
                    c = [mark(v.tensor_scalar(src[:, t, :], src[:, t, :], rscale[:, i, t:t + 1], QMAX, ALU.mult, ALU.min)) for t in ts]
                    for k, t in enumerate(ts):
                        after(c[k])
                        c[k] = mark(v.tensor_scalar(src[:, t, :], src[:, t, :], -QMAX, ROUND, ALU.max, ALU.add))
                    for k, t in enumerate(ts):
                        after(c[k])
                        v.tensor_scalar(dst[:, t, :], src[:, t, :], ROUND, None, ALU.subtract).then_inc(s[done], 1)

            def key_lo(i):
                acc, rows, other, cols, bias = key_half(i)
                dve.wait_ge(s["k_hi"], i + 1)
                v.scalar_tensor_tensor(key[other, cols], acc, bias, fr(key[rows, cols]),
                                       ALU.add, ALU.subtract).then_inc(s["k_lo"], 1)

            def query(i):
                dve.wait_ge(s["q_mm"], i + 1)
                if i == 0:
                    dve.wait_ge(s["q_scales"], 2)
                v.scalar_tensor_tensor(q_f[:, i, :], bank(i), wq_scale_col[:, i:i + 1], x_scale_all[:],
                                       ALU.mult, ALU.mult).then_inc(s["q_f"], 1)

            def query_lo(i):
                dve.wait_ge(s["q_hi"], i + 1)
                at = slice(i * TOK, (i + 1) * TOK)
                v.scalar_tensor_tensor(q_lo[:, at], q_f[:, i, :], bq_sb[:, i:i + 1], fr(q_hi[:, at]),
                                       ALU.add, ALU.subtract).then_inc(s["q_lo"], 1)

            dve.wait_ge(ld["x"], 16)
            layer_norm(x_sb, 0)
            dve.wait_ge(s["xn1"], NT)
            quantise(xn[:], 0, NT, xq, "xq")
            dve.wait_ge(ld["wq"], 16)
            quantise(wq_sb[:], 1, CK, wqq, "wqq")
            dve.wait_ge(ld["bq"], 32)
            after(mark(v.tensor_scalar(bq_sb[:], bq_sb[:], float(D) ** -0.5, None, ALU.mult)))
            for i in range(G * B):
                if i == 4:
                    dve.wait_ge(s["rows"], 1)
                    v.tensor_copy(wqq_t[:], twice(bank_bf(5, CK * C))).then_inc(s["wqq_t"], 1)
                key_lo(i)
            query(0)
            query(1)
            query_lo(0)
            for i in range(2, G):
                query(i)
            for i in range(1, G):
                query_lo(i)

            dve.wait_ge(ld["mask"], 16)

            def add_mask(h, t):
                n = h * NT + t
                dve.wait_ge(s["score"], n + 1)
                wait(dve, "expd", n - 3)
                dve.sem_inc(s["sm_turn"], 1)
                v.tensor_tensor_reduce(neg_s[:, t, :], bank(t % 2), mask_sb[:, t, :], -1.0, BIG, ALU.add, ALU.min,
                                       neg_max[:, t:t + 1]).then_inc(s["sm"], 1)

            def transposed_lo(h, t):
                n = h * NT + t
                dve.wait_ge(s["pt_hi"], n + 1)
                hi = pt_cols(pt_hi, t)
                v.tensor_tensor(pt_cols(pt_lo, t), pt_bank(t), fr(hi), ALU.subtract).then_inc(s["pt_lo"], 1)

            def gather_out(gr):
                dve.wait_ge(s["expd"], (gr + 1) * (HG * NT))
                sums = p_sum[:, :, bass.ds(gr * HG, HG)]
                v.reciprocal(sums, sums).then_inc(s["p_inv"], 1)
                dve.wait_ge(s["p_inv"], gr + 1)
                dve.wait_ge(s["out_tp"], gr + 1)
                dve.sem_inc(s["sm_turn"], 1)
                dst = o_sb[:, :, bass.ds(gr * GC, GC)].rearrange("p t (h d) -> p t h d", d=D)
                v.tensor_tensor(dst, bank(7, NT * GC).rearrange("p (t h d) -> p t h d", t=NT, d=D),
                                sums.unsqueeze(3).to_broadcast([P, NT, HG, D]), ALU.mult).then_inc(s["out_got"], 1)

            def group(gr, first=False):
                for hh in range(HG):
                    h = gr * HG + hh
                    for t in range(NT):
                        add_mask(h, t)
                        if first and hh == 0 and t == 1:
                            dve.wait_ge(ld["wo"], 16)
                            quantise(wo_sb[:], 2, CK, woq, "woq")
                        if not (first and hh == 0):
                            transposed_lo(h - 1, t)
                        if hh == 2 and t == 1 and not first:
                            gather_out(gr - 1)

            dve.wait_ge(s["q_lo"], G)
            dve.sem_inc(s["out_got"], 1)
            group(0, True)
            with dve.Fori(1, G) as gr:
                group(gr)
            for t in range(NT):
                transposed_lo(H - 1, t)
            dve.wait_ge(s["out_got"], G)
            mark(v.tensor_reduce(o_max[:, 0, :], o_sb[:, :, 0:C - GC], AX.X, ALU.max, apply_absolute_value=True))
            dve.wait_ge(s["const_sel"], 1)
            v.tensor_scalar(expert_sel[:], expert_of[:], part_mod[:, 0:1], None, ALU.is_equal).then_inc(s["sel"], 1)
            gather_out(G - 1)

            dve.wait_ge(s["out_got"], G + 1)
            after(mark(v.tensor_reduce(o_max[:, 1, :], o_sb[:, :, C - GC:C], AX.X, ALU.max, apply_absolute_value=True)))
            after(mark(v.tensor_tensor(amax[:, 3, :], o_max[:, 0, :], o_max[:, 1, :], ALU.max)))
            quantise(o_sb[:], 3, NT, oq, "oq", amax_found=True)
            dve.wait_ge(s["wo_sc"], 1)
            for t in range(NT):
                dve.wait_ge(s["o_mm"], t + 1)
                v.scalar_tensor_tensor(proj[:, t, :], bank(2 + t % 2, C), scale[:, 3, t:t + 1], wo_scale[:],
                                       ALU.mult, ALU.mult).then_inc(s["o_read"], 1)
            layer_norm(x2, 1)

            for t in range(NT):
                at = slice(t * P, (t + 1) * P)
                dve.wait_ge(s["xn_hi"], t + 1)
                v.tensor_tensor(xn_lo[:, :, at], xn_t[:, :, at], fr(xn_hi[:, :, at]), ALU.subtract).then_inc(s["xn_lo"], 1)

            def gate_up(j, sl):
                dve.wait_ge(s["u_mm"], j + 1)
                dve.wait_ge(s["silu"], j + 1)
                v.tensor_tensor(gated[:, sl, :], silu[:, sl, :], bank(2 + sl), ALU.mult).then_inc(s["gated"], 1)

            def weigh(j, sl):
                dve.wait_ge(s["gated"], j + 1)
                dve.wait_ge(s["ce_mm"], j + 1)
                wait(dve, "hid_hi", j - 1)
                v.tensor_tensor(hid[:, sl, :], gated[:, sl, :], bank(4 + sl), ALU.mult).then_inc(s["hid"], 1)

            def hidden_lo(j, sl):
                dve.wait_ge(s["hid_hi"], j + 1)
                wait(dve, "dn_mm", j - 1)
                v.tensor_tensor(hid_lo[:, sl, :], hid[:, sl, :], fr(hid_hi[:, sl, :]), ALU.subtract).then_inc(s["hid_lo"], 1)

            r = lambda ap: ap.unsqueeze(2)
            dve.wait_ge(s["lg_mm"], NT)
            lg = bank(6, NT * E).rearrange("p (t e) -> p t e", t=NT)
            after(mark(v.tensor_reduce(r_max[:], lg, AX.X, ALU.max)))
            v.tensor_tensor(r_e[:], lg, r(r_max[:]).to_broadcast([P, NT, E]), ALU.subtract).then_inc(s["lg_sub"], 1)
            dve.wait_ge(s["lg_exp"], 1)
            after(mark(v.tensor_reduce(r_sum[:, 0, :], r_e[:], AX.X, ALU.add)))
            after(mark(v.reciprocal(r_sum[:, 0, :], r_sum[:, 0, :])))
            dve.wait_ge(s["const_pad"], 1)
            v.tensor_tensor(r_p[:, :, 0:E], r_e[:], r(r_sum[:, 0, :]).to_broadcast([P, NT, E]), ALU.mult).then_inc(s["r_p"], 1)
            dve.wait_ge(s["r_p"], 1)
            for t in range(NT):
                c = mark(v.max(r_top[:, t, :], r_p[:, t, 0:E]))
            after(c)

            def inverse_sum(src, row):
                total = r_sum[:, row, :]
                after(mark(v.tensor_reduce(total, src, AX.X, ALU.add)))
                after(mark(v.tensor_scalar(total, total, 1e-12, None, ALU.max)))
                after(mark(v.reciprocal(total, total)))

            inverse_sum(r_top[:], 1)
            after(mark(v.tensor_tensor(r_ren[:], r_top[:], r(r_sum[:, 1, :]).to_broadcast([P, NT, TOPK]), ALU.mult)))
            for t in range(NT):
                c = mark(v.tensor_tensor_scan(r_cum[:, t, :], r_ren[:, t, :], r_zero[:], 0.0, ALU.add, ALU.add))
            after(c)
            after(mark(v.tensor_scalar(r_act[:, :, 1:TOPK], r_cum[:, :, 0:TOPK - 1], KEEP, None, ALU.is_lt)))
            after(mark(v.tensor_tensor(r_rw[:], r_top[:], r_act[:], ALU.mult)))
            after(mark(v.scalar_tensor_tensor(r_find[:], r_act[:], -1.0, r_rw[:], ALU.add, ALU.add)))
            for t in range(NT):
                mark(v.match_replace(r_rep[:, t, :], r_find[:, t, :], r_p[:, t, :], -2.0))
            after(n[0])
            for part, p in enumerate((r_p[:, :, 0:E], p_rest[:, 0], p_rest[:, 1])):
                if part:
                    dve.wait_ge(s["p_rest"], part)
                v.scalar_tensor_tensor(comb3[:, :, part, :], r_rep[:, :, 0:E], -1.5, p,
                                       ALU.is_lt, ALU.mult).then_inc(s["comb"], 1)
            gate_up(0, 0)
            inverse_sum(r_rw[:], 2)

            gate_up(1, 1)
            weigh(0, 0)
            weigh(1, 1)
            hidden_lo(0, 0)
            hidden_lo(1, 1)
            gate_up(2, 0)
            def expert_step(j, sl):
                gate_up(j, sl)
                weigh(j - 1, 1 - sl)
                hidden_lo(j - 1, 1 - sl)

            expert_step(3, 1)
            with dve.Fori(2, FT // 2 - 1) as i:
                for sl in range(2):
                    expert_step(i * 2 + sl, sl)
            expert_step(FT - 2, 0)
            weigh(FT - 2, 0)
            hidden_lo(FT - 2, 0)
            gate_up(FT - 1, 1)
            weigh(FT - 1, 1)
            hidden_lo(FT - 1, 1)
            for t in range(NT):
                dve.wait_ge(s["y_mm"], t // 2 * 2 + 2)
                v.scalar_tensor_tensor(y_sb[:, t, :], ps[:, 6 + t // 2, (t % 2) * C:(t % 2 + 1) * C], r_sum[:, 2, t:t + 1],
                                       x2[:, t, :], ALU.mult, ALU.add).then_inc(s["y_done"], 1)

        @block.tensor
        def _(pe):
            mm = nc.tensor.matmul

            def product(acc, terms):
                for i, (lhs, rhs) in enumerate(terms):
                    ins = mm(acc, lhs, rhs, start=(i == 0), stop=(i == len(terms) - 1))
                return ins

            def key_proj(b):
                cols = slice(b * L, (b + 1) * L)
                for m, (w, c) in enumerate(((wk_hi, ctx_hi), (wk_lo, ctx_hi), (wk_hi, ctx_lo))):
                    if m == 1 and b == 0:
                        pe.wait_ge(s["wk_lo"], 1)
                    if m == 2:
                        pe.wait_ge(s["ctx_lo"], CK * (b + 1))
                    for pair in range(CK):
                        for k in range(CK):
                            ins = mm(bank(b * CK + pair), w[:, k, pair * P:(pair + 1) * P], c[:, k, cols],
                                     start=(m == 0 and k == 0), stop=(m == 2 and k == CK - 1))
                        if m == 2:
                            ins.then_inc(s["k_mm"], 1)

            def transposes(dst, src, tiles):
                for t in range(tiles):
                    for k in range(CK):
                        ins = nc.tensor.transpose(dst[:, k, t * P:(t + 1) * P], src[:, t, k * P:(k + 1) * P], ident_bf[:])
                return ins

            def value_proj(i):
                wait(pe, "v_sb", i - 1)
                at = slice(i * P, (i + 1) * P)
                product(bank(V_BANKS[i % 2], C), [
                    (c[:, k, at], w[:, k, :])
                    for k in range(CK) for w, c in ((wv_hi, ctx_hi), (wv_lo, ctx_hi), (wv_hi, ctx_lo))
                ]).then_inc(s["v_mm"], 1)

            pe.wait_ge(s["wk_hi"], 1)
            pe.wait_ge(s["ctx_hi"], 1)
            key_proj(0)
            pe.wait_ge(s["const_ident"], 3)
            pe.wait_ge(s["xq"], 1)
            for t in range(NT):
                ins = nc.tensor.transpose(ps[0:1, 5, t * P:(t + 1) * P], scale[:, 0, t:t + 1], ident[:])
            ins.then_inc(s["x_row_tp"], 1)
            pe.wait_ge(s["ctx_hi"], 2)
            key_proj(1)
            pe.wait_ge(s["x_row"], 1)
            mm(bank(6), ones_row[:], x_scale_row[:], start=True, stop=True).then_inc(s["x_scale_mm"], 1)
            pe.wait_ge(s["xq"], NT)
            transposes(bank_bf(4, CK * TOK).rearrange("p (k n) -> p k n", k=CK), xq, NT).then_inc(s["xq_tp"], 1)
            pe.wait_ge(s["wqq"], CK)
            transposes(bank_bf(5, CK * C).rearrange("p (k n) -> p k n", k=CK), wqq, CK)
            for k in range(CK):
                ins = nc.tensor.transpose(ps[0:1, 5, C + k * P:C + (k + 1) * P], scale[:, 1, k:k + 1], ident[:])
            ins.then_inc(s["w_tp"], 1)
            pe.wait_ge(s["wv_lo"], 1)
            value_proj(0)
            pe.wait_ge(s["xq_t"], 1)
            value_proj(1)
            pe.wait_ge(s["rows"], 1)
            pe.wait_ge(s["wqq_t"], 1)
            for i in range(G):
                ins = mm(ps[:, 5, i:i + 1], wq_scale_row[:, i].rearrange("p a c -> p (a c)"), ones_row[:, 0:1], start=True, stop=True)
            ins.then_inc(s["q_scales_mm"], 1)
            for i in range(G):
                pe.wait_ge(s["k_lo"], 2 * i + 2)
                product(bank(i), [(wqq_t[:, k * G + i].rearrange("p a c -> p (a c)"), xq_t[:, k, :]) for k in range(CK)]).then_inc(s["q_mm"], 1)
            for i in range(2, V_EARLY):
                value_proj(i)

            def scores(h, t):
                n = h * NT + t
                pe.wait_ge(s["qm"], h * (NT // 2) + (t // 2 + 1))
                wait(pe, "sm", n - 1)
                kb = key[:, group_at(h, B * L, t // NTB * L, L)]
                at = slice(t * P, (t + 1) * P)
                product(bank(t % 2), [(qm_hi[:, at], kb), (qm_lo[:, at], kb)]).then_inc(s["score"], 1)

            def transpose_probs(h, t):
                n = h * NT + t
                pe.wait_ge(s["expd"], n + 1)
                wait(pe, "pt_lo", n - 3)
                if isinstance(n, int) and n == PT_BANKS.index(V_BANKS[1]):
                    pe.wait_ge(s["v_sb"], B * LC)
                for k in range(LC):
                    at = slice(k * P, (k + 1) * P)
                    ins = nc.tensor.transpose(ps[:, PT_BANKS[t], at], prob[:, t, at], ident[:])
                ins.then_inc(s["pt_mm"], 1)

            def values(h, hh, b):
                pe.wait_ge(s["pt_lo"], h * NT + (b * NTB + NTB))
                pe.wait_ge(s["v_split"], h + 1)
                for k in range(LC):
                    for pt in (pt_hi, pt_lo):
                        ins = mm(ps[:, 5, b * N:(b + 1) * N], val_head[:, hh, b * LC + k], pt[:, b, k, :],
                                 start=(hh == 0 and b == 0 and k == 0 and pt is pt_hi),
                                 stop=(hh == HG - 1 and k == LC - 1 and pt is pt_lo), skip_group_check=True)
                ins.then_inc(s["pv"], 1)

            def transpose_out(gr):
                pe.wait_ge(s["ot"], gr + 1)
                pe.wait_ge(s["out_got"], gr + 1)
                for t in range(NT):
                    ins = mm(ps[:, 7, t * GC:(t + 1) * GC], ot_sb[:, t * P:(t + 1) * P], hi_lo_sum[:], start=True, stop=True)
                ins.then_inc(s["out_tp"], 1)

            def group(gr, first=False):
                for hh in range(HG):
                    h = gr * HG + hh
                    start = first and hh == 0
                    for t in range(NT):
                        scores(h, t)
                        if start and V_EARLY + t < B * LC:
                            value_proj(V_EARLY + t)
                        if t == 1 and not (first and hh < 2):
                            values(h - 2, (hh - 2) % HG, 1)
                        later = hh == 1 and not first
                        if t == 3 and not start and not later:
                            values(h - 1, (hh - 1) % HG, 0)
                        if t >= 2:
                            transpose_probs(h, t - 2)
                            if t == 3 and later:
                                pe.wait_ge(s["ot"], gr)
                                values(h - 1, (hh - 1) % HG, 0)
                        elif not start:
                            transpose_probs(h - 1, t + 2)
                        if hh == 2 and t == 0 and not first:
                            transpose_out(gr - 1)

            pe.wait_ge(s["q_f"], G)
            group(0, True)
            with pe.Fori(1, G) as gr:
                group(gr)
            transpose_probs(H - 1, 2)
            values(H - 2, HG - 2, 1)
            transpose_probs(H - 1, 3)
            values(H - 1, HG - 1, 0)
            values(H - 1, HG - 1, 1)
            transpose_out(G - 1)

            def keep_clock(n):
                for _ in range(n):
                    mm(bank(7), ident_bf[:], woq_t[:].rearrange("p k n -> p (k n)"), start=True, stop=True)

            def out_proj(t):
                pe.wait_ge(s["oq_t"], t + 1)
                wait(pe, "o_read", t - 1)
                product(bank(2 + t % 2, C), [(oq_t[:, t, k, :], woq_t[:, k, :]) for k in range(CK)]).then_inc(s["o_mm"], 1)

            def logits(t):
                pe.wait_ge(s["xn_t"], t + 1)
                for k in range(CK):
                    ins = mm(ps[:, 6, t * E:(t + 1) * E], xn_t[:, k, t * P:(t + 1) * P], gate_sb[:, k, :],
                             start=(k == 0), stop=(k == CK - 1))
                ins.then_inc(s["lg_mm"], 1)

            pe.wait_ge(s["woq"], CK)
            pe.wait_ge(s["pt_lo"], H * NT)
            transposes(bank_bf(2, CK * C).rearrange("p (k n) -> p k n", k=CK), woq, CK).then_inc(s["wo_tp"], 1)
            for k in range(CK):
                ins = nc.tensor.transpose(ps[0:1, 3, k * P:(k + 1) * P], scale[:, 2, k:k + 1], ident[:])
            ins.then_inc(s["wo_row_tp"], 1)
            pe.wait_ge(s["wo_row"], 1)
            mm(bank(4, C), ones_row[:], wo_scale_row[:], start=True, stop=True).then_inc(s["wo_sc_mm"], 1)
            pe.wait_ge(s["wo_sc"], 1)

            for t in range(NT):
                pe.wait_ge(s["oq"], t + 1)
                wait(pe, "oq_t", t - 1)
                tp = bank_bf(t % 2, CK * P).rearrange("p (k n) -> p k n", k=CK)
                for k in range(CK):
                    ins = nc.tensor.transpose(tp[:, k, :], oq[:, t, k * P:(k + 1) * P], ident_bf[:])
                ins.then_inc(s["oq_tp"], 1)
                if t:
                    out_proj(t - 1)
            out_proj(NT - 1)
            keep_clock(FILLERS)

            pe.wait_ge(ld["gate"], 16)
            for t in range(NT):
                pe.wait_ge(s["xn2"], t + 1)
                for k in range(CK):
                    ins = nc.tensor.transpose(ps[:, XT_BANKS[t], k * P:(k + 1) * P], xn[:, t, k * P:(k + 1) * P], ident[:])
                ins.then_inc(s["xn_tp"], 1)
                if t > 1:
                    logits(t - 2)
            logits(NT - 2)
            logits(NT - 1)

            parts = ((0, "silu", "g_mm"), (1, "gated", "u_mm"))

            def gate_and_up(j, sl, parts=parts):
                pe.wait_ge(s["gu_split"], j + 1)
                for u, freed, done in parts:
                    wait(pe, freed, j - 1)
                    product(bank(2 * u + sl), [
                        (w[:, sl, (2 * k + u) * P:(2 * k + u + 1) * P], xt[:, k, :])
                        for k in range(CK) for w, xt in ((w_hi_gu, xn_hi), (w_lo_gu, xn_hi), (w_hi_gu, xn_lo))
                    ]).then_inc(s[done], 1)

            def token_weights(j, sl):
                wait(pe, "hid", j - 1)
                mm(bank(4 + sl), expert_sel[0:3 * E, bass.ds(j * P, P)], comb_part[0:3 * E, :], start=True, stop=True).then_inc(s["ce_mm"], 1)

            def down(j, sl, first=False, last=False):
                pe.wait_ge(s["hid_lo"], j + 1)
                pe.wait_ge(s["dn_split"], j + 1)
                for t in range(NT):
                    at = slice(t * P, (t + 1) * P)
                    acc = ps[:, 6 + t // 2, (t % 2) * C:(t % 2 + 1) * C]
                    terms = ((hid_hi, w_hi_dn), (hid_hi, w_lo_dn), (hid_lo, w_hi_dn))
                    for i, (hd, w) in enumerate(terms):
                        ins = mm(acc, hd[:, sl, at], w[:, sl, :], start=(first and i == 0 and t % 2 == 0),
                                 stop=(last and i == 2), skip_group_check=True)
                    if last:
                        ins.then_inc(s["y_mm"], 1)
                if not last:
                    ins.then_inc(s["dn_mm"], 1)

            pe.wait_ge(s["xn_lo"], NT)
            gate_and_up(0, 0)
            gate_and_up(1, 1)
            gate_and_up(2, 0, parts[:1])
            pe.wait_ge(s["comb"], 3)
            for t in range(NT):
                ins = nc.tensor.transpose(bank_bf(7, TOK)[0:3 * E, t * P:(t + 1) * P], comb3[:, t].rearrange("p a e -> p (a e)"), ident_bf[:])
            ins.then_inc(s["comb_tp"], 1)
            gate_and_up(2, 0, parts[1:])
            pe.wait_ge(s["comb_part"], 1)
            pe.wait_ge(s["sel"], 1)
            token_weights(0, 0)
            token_weights(1, 1)
            gate_and_up(3, 1)
            down(0, 0, first=True)
            token_weights(2, 0)
            down(1, 1)
            def expert_step(j, sl):
                gate_and_up(j, sl)
                token_weights(j - 1, 1 - sl)
                down(j - 2, sl)

            with pe.Fori(2, FT // 2 - 1) as i:
                for sl in range(2):
                    expert_step(i * 2 + sl, sl)
            expert_step(FT - 2, 0)
            token_weights(FT - 2, 0)
            gate_and_up(FT - 1, 1)
            token_weights(FT - 1, 1)
            down(FT - 3, 1)
            down(FT - 2, 0)
            down(FT - 1, 1, last=True)


def kernel(**inputs):
    import numpy as np
    import concourse.bacc as bacc
    from concourse.bass_utils import run_bass_kernel_spmd

    a = {k: np.asarray(v) for k, v in inputs.items()}
    gu = a["L0_ffn_gate_up_proj"].reshape(E, 2, INTER, CK, P)
    gu = gu.transpose(4, 3, 1, 0, 2).reshape(P, CK, 2, FT, P)
    arrays = {
        "x": a["x"].reshape(TOK, C),
        "ctx_t": a["ctx_2048"].reshape(B * L, C).T,
        "mask": a["mask_BxSxS2_ff0"],
        "wq": a["L0_xattn_wq"],
        "bq_t": a["L0_xattn_bq"].reshape(G, GC).T,
        "wk_t": a["L0_xattn_wk"].T,
        "bk_t": a["L0_xattn_bk"].reshape(CK, P).T,
        "wv_t": a["L0_xattn_wv"].T,
        "bv": a["L0_xattn_bv"],
        "wo": a["L0_xattn_wo"],
        "bo": a["L0_xattn_bo"],
        "gate_t": a["L0_ffn_gate_weight"].T,
        "gu_t": gu.transpose(0, 3, 1, 2, 4).reshape(P, FT, WGU),
        "down_t": a["L0_ffn_down_proj"].transpose(0, 2, 1).reshape(FT, P, C).transpose(1, 0, 2),
    }
    nc = bacc.Bacc("TRN2", target_bir_lowering=False, num_devices=1)
    arrays = {f"in_{k}": np.ascontiguousarray(v) for k, v in arrays.items()}
    args = [nc.dram_tensor(k, v.shape, mybir.dt.from_np(v.dtype), kind="ExternalInput").ap() for k, v in arrays.items()]
    out = nc.dram_tensor("out_0", (B, N, C), F32, kind="ExternalOutput").ap()
    build(nc, *args, out)
    return run_bass_kernel_spmd(nc, [arrays], core_ids=[0]).results[0]["out_0"]
```
